# Optimizing a Trainium2 kernel written in Bass

```python
import numpy as np
import jax
import jax.numpy as jnp

def _softmax(x, axis=-1):
    return jax.nn.softmax(x, axis=axis)

def _gelu(x):
    return jax.nn.gelu(x, approximate=True)

def _silu(x):
    return jax.nn.silu(x)

def _sigmoid(x):
    return jax.nn.sigmoid(x)

def _layernorm(x, axis=-1, eps=1e-05):
    m = jnp.mean(x, axis=axis, keepdims=True)
    v = jnp.var(x, axis=axis, keepdims=True)
    return (x - m) / jnp.sqrt(v + eps)

def _scatter_add(tgt, idx, src, axis=0):
    return tgt.at[idx].add(src)

def _segment_sum(src, seg, n):
    return jax.ops.segment_sum(src, seg, n)
kernel_name = 'mk_gnn_resnorm_d2_gnn_r8_f12e94'

def setup_inputs(seed: int=0):
    np.random.seed(seed)
    _w = jnp.asarray

    def _rec_inputs():
        import jax
        import jax.numpy as jnp
        _gk = jax.random.key(seed)
        x = -0.0003713 + 1 * jax.random.normal(jax.random.fold_in(_gk, 1), (12500, 256), jnp.float32)
        src = jax.random.randint(jax.random.fold_in(_gk, 2), (200000,), 0, 12500, jnp.int32)
        dst = jnp.minimum((12500 * jax.random.uniform(jax.random.fold_in(_gk, 3), (200000,)) ** 2.0).astype(jnp.int32), 99999)
        _o = jnp.argsort(dst, stable=True)
        src = src[_o]
        dst = dst[_o]
        return (x, src, dst)
    x, src, dst = _rec_inputs()

    def _L0_gnn_setup():
        import jax, jax.numpy as jnp
        import numpy as np
        N, E = (6250, 100000)
        H, C_IN, C_HID, C_OUT = (4, 256, 64, 64)
        NEG_SLOPE = 0.2

        def leaky_relu(x, s=NEG_SLOPE):
            return jnp.where(x >= 0, x, s * x)

        def gat_conv(x, src, dst, W, att_src, att_dst, bias, n_nodes):
            Hh, Cc = (att_src.shape[1], att_src.shape[2])
            h = (x @ W).reshape(n_nodes, Hh, Cc)
            a_src = (h * att_src).sum(-1)
            a_dst = (h * att_dst).sum(-1)
            alpha = leaky_relu(a_src[src] + a_dst[dst])
            m = jax.ops.segment_max(alpha, dst, num_segments=n_nodes)
            e = jnp.exp(alpha - m[dst])
            denom = jax.ops.segment_sum(e, dst, num_segments=n_nodes)
            w = e / jnp.clip(denom, 1e-16)[dst]
            out = jax.ops.segment_sum(w[:, :, None] * h[src], dst, num_segments=n_nodes)
            return out.reshape(n_nodes, Hh * Cc) + bias
        key = jax.random.key(seed)
        ks = jax.random.split(key, 10)
        glorot = lambda k, shp: jax.random.normal(k, shp, jnp.float32) * np.sqrt(2.0 / (shp[0] + shp[-1]))
        return {'x': jax.random.normal(ks[0], (N, C_IN), jnp.float32), 'edge_index': jax.random.randint(ks[1], (2, E), 0, N, jnp.int32), 'W1': glorot(ks[2], (C_IN, H * C_HID)), 'att_src1': glorot(ks[3], (1, H, C_HID)), 'att_dst1': glorot(ks[4], (1, H, C_HID)), 'b1': jnp.zeros((H * C_HID,), jnp.float32), 'W2': glorot(ks[5], (H * C_HID, H * C_OUT)), 'att_src2': glorot(ks[6], (1, H, C_OUT)), 'att_dst2': glorot(ks[7], (1, H, C_OUT)), 'b2': jnp.zeros((H * C_OUT,), jnp.float32)}
    _L0_gnn_all = _L0_gnn_setup()
    _L0_gnn_in = {k: v for k, v in _L0_gnn_all.items() if k in ('W1', 'att_src1', 'att_dst1', 'b1', 'W2', 'att_src2', 'att_dst2', 'b2')}
    del _L0_gnn_all

    def _L1_gnn_setup():
        import jax, jax.numpy as jnp
        import numpy as np
        N_NODES = 6250
        N_EDGES = 100000
        IN_DIM = 256
        OUT_DIM = 32
        NUM_HEADS = 8
        key = jax.random.key(seed)
        ks = jax.random.split(key, 9)
        h = jax.random.normal(ks[0], (N_NODES, IN_DIM), dtype=jnp.float32)
        src = jax.random.randint(ks[1], (N_EDGES,), 0, N_NODES, dtype=jnp.int32)
        dst = jax.random.randint(ks[2], (N_EDGES,), 0, N_NODES, dtype=jnp.int32)
        s = 1.0 / np.sqrt(IN_DIM)
        W_lin = jax.random.uniform(ks[3], (IN_DIM, IN_DIM), jnp.float32, -s, s)
        b_lin = jax.random.uniform(ks[4], (IN_DIM,), jnp.float32, -s, s)
        W_gat = jax.random.normal(ks[5], (IN_DIM, NUM_HEADS * OUT_DIM), dtype=jnp.float32) * s
        attn_l = jax.random.normal(ks[6], (NUM_HEADS, OUT_DIM), dtype=jnp.float32) * 0.1
        attn_r = jax.random.normal(ks[7], (NUM_HEADS, OUT_DIM), dtype=jnp.float32) * 0.1
        gat_bias = jnp.zeros((NUM_HEADS * OUT_DIM,), dtype=jnp.float32)
        return {'h': h, 'src': src, 'dst': dst, 'W_lin': W_lin, 'b_lin': b_lin, 'W_gat': W_gat, 'attn_l': attn_l, 'attn_r': attn_r, 'gat_bias': gat_bias}
    _L1_gnn_all = _L1_gnn_setup()
    _L1_gnn_in = {k: v for k, v in _L1_gnn_all.items() if k in ('W_lin', 'b_lin', 'W_gat', 'attn_l', 'attn_r', 'gat_bias')}
    del _L1_gnn_all
    return {'x': x, 'src': src, 'dst': dst, 'L0_gnn_W1': _L0_gnn_in['W1'], 'L0_gnn_att_src1': _L0_gnn_in['att_src1'], 'L0_gnn_att_dst1': _L0_gnn_in['att_dst1'], 'L0_gnn_b1': _L0_gnn_in['b1'], 'L0_gnn_W2': _L0_gnn_in['W2'], 'L0_gnn_att_src2': _L0_gnn_in['att_src2'], 'L0_gnn_att_dst2': _L0_gnn_in['att_dst2'], 'L0_gnn_b2': _L0_gnn_in['b2'], 'L1_gnn_W_lin': _L1_gnn_in['W_lin'], 'L1_gnn_b_lin': _L1_gnn_in['b_lin'], 'L1_gnn_W_gat': _L1_gnn_in['W_gat'], 'L1_gnn_attn_l': _L1_gnn_in['attn_l'], 'L1_gnn_attn_r': _L1_gnn_in['attn_r'], 'L1_gnn_gat_bias': _L1_gnn_in['gat_bias']}

def reference(x, src, dst, L0_gnn_W1, L0_gnn_att_src1, L0_gnn_att_dst1, L0_gnn_b1, L0_gnn_W2, L0_gnn_att_src2, L0_gnn_att_dst2, L0_gnn_b2, L1_gnn_W_lin, L1_gnn_b_lin, L1_gnn_W_gat, L1_gnn_attn_l, L1_gnn_attn_r, L1_gnn_gat_bias):
    import jax
    import jax.numpy as jnp

    def _L0_gnn_ref(x, edge_index, W1, att_src1, att_dst1, b1, W2, att_src2, att_dst2, b2):
        import jax, jax.numpy as jnp
        import numpy as np
        N, E = (6250, 100000)
        H, C_IN, C_HID, C_OUT = (4, 256, 64, 64)
        NEG_SLOPE = 0.2

        def leaky_relu(x, s=NEG_SLOPE):
            return jnp.where(x >= 0, x, s * x)

        def gat_conv(x, src, dst, W, att_src, att_dst, bias, n_nodes):
            Hh, Cc = (att_src.shape[1], att_src.shape[2])
            h = (x @ W).reshape(n_nodes, Hh, Cc)
            a_src = (h * att_src).sum(-1)
            a_dst = (h * att_dst).sum(-1)
            alpha = leaky_relu(a_src[src] + a_dst[dst])
            m = jax.ops.segment_max(alpha, dst, num_segments=n_nodes)
            e = jnp.exp(alpha - m[dst])
            denom = jax.ops.segment_sum(e, dst, num_segments=n_nodes)
            w = e / jnp.clip(denom, 1e-16)[dst]
            out = jax.ops.segment_sum(w[:, :, None] * h[src], dst, num_segments=n_nodes)
            return out.reshape(n_nodes, Hh * Cc) + bias
        n = x.shape[0]
        loops = jnp.arange(n, dtype=edge_index.dtype)
        src = jnp.concatenate([edge_index[0], loops])
        dst = jnp.concatenate([edge_index[1], loops])
        h1 = gat_conv(x, src, dst, W1, att_src1, att_dst1, b1, n)
        h1 = jax.nn.relu(h1)
        out = gat_conv(h1, src, dst, W2, att_src2, att_dst2, b2, n)
        return out

    def _L1_gnn_ref(h, src, dst, W_lin, b_lin, W_gat, attn_l, attn_r, gat_bias):
        import jax, jax.numpy as jnp
        import numpy as np
        N_NODES = 6250
        N_EDGES = 100000
        IN_DIM = 256
        OUT_DIM = 32
        NUM_HEADS = 8
        N = h.shape[0]
        h = h @ W_lin + b_lin
        h_in = h
        feat = (h @ W_gat).reshape(N, NUM_HEADS, OUT_DIM)
        el = jnp.sum(feat * attn_l, axis=-1)
        er = jnp.sum(feat * attn_r, axis=-1)
        e = jax.nn.leaky_relu(el[src] + er[dst], 0.2)
        m = jax.ops.segment_max(e, dst, num_segments=N)
        m = jnp.where(jnp.isfinite(m), m, 0.0)
        e = jnp.exp(e - m[dst])
        s = jax.ops.segment_sum(e, dst, num_segments=N)
        a = e / s[dst]
        msg = feat[src] * a[:, :, None]
        out = jax.ops.segment_sum(msg, dst, num_segments=N)
        out = out.reshape(N, NUM_HEADS * OUT_DIM) + gat_bias
        out = jax.nn.leaky_relu(out, 0.01)
        return h_in + out
    edge_index = jnp.stack([src, dst])
    x = _layernorm(x + _L0_gnn_ref(x, edge_index, L0_gnn_W1, L0_gnn_att_src1, L0_gnn_att_dst1, L0_gnn_b1, L0_gnn_W2, L0_gnn_att_src2, L0_gnn_att_dst2, L0_gnn_b2), axis=-1)
    x = _layernorm(x + _L1_gnn_ref(x, src, dst, L1_gnn_W_lin, L1_gnn_b_lin, L1_gnn_W_gat, L1_gnn_attn_l, L1_gnn_attn_r, L1_gnn_gat_bias), axis=-1)
    return x

_drawn_inputs = setup_inputs


def setup_inputs(seed=0):
    import zlib

    import numpy as np

    out = dict(_drawn_inputs(seed))
    spreads = {'L0_gnn_b1': (0.0, 0.1), 'L0_gnn_b2': (0.0, 0.1), 'L1_gnn_gat_bias': (0.0, 0.1)}
    factors = {'L0_gnn_att_dst1': 2.853,
     'L0_gnn_att_dst2': 182.763,
     'L1_gnn_attn_r': 93.671,
     'L0_gnn_att_src2': 2.702}
    for name, (base, spread) in spreads.items():
        noise = np.random.default_rng([zlib.crc32(name.encode()), seed]).standard_normal(out[name].shape)
        drawn = base * np.exp(spread * noise) if base else spread * noise
        out[name] = jnp.asarray(drawn.astype(out[name].dtype))
    for name, factor in factors.items():
        out[name] = (out[name] * factor).astype(out[name].dtype)
    return out
```

```python
import concourse.bass as bass
from concourse import mybir
from contextlib import ExitStack

F32 = mybir.dt.float32
BF16 = mybir.dt.bfloat16
I32 = mybir.dt.int32
ALU = mybir.AluOpType
ACT = mybir.ActivationFunctionType
AX = mybir.AxisListType
ENG = mybir.EngineType

P = 128
N_NODES = 12500
N_EDGES = 200000
D = 256
TILES = -(-N_EDGES // P)
BLOCKS = -(-N_NODES // P)
NODES_PAD = BLOCKS * P
EDGES_PAD = TILES * P
G = 16
WINDOWS = -(-(TILES + BLOCKS - 1) // G)
WINDOWS += WINDOWS % 2
STEPS = WINDOWS * G
SG = STEPS // P
assert STEPS == SG * P
ACC_W = D + 16
ADS_W = 24
MASKS = 5
BIG = 1e30
SLOPE = 0.2
OUT_SLOPE = 0.01
EPS = 1e-5


def build_program(nc, t, debug=None):
    top = ExitStack()

    def sbuf(stack, name, shape, dtype):
        return stack.enter_context(nc.sbuf_tensor(name, shape, dtype))

    def psum(stack, name, shape, dtype=F32):
        return stack.enter_context(nc.psum_tensor(name, shape, dtype))

    def sem(name):
        return top.enter_context(nc.semaphore(name))

    table = [nc.dram_tensor(f"table{L}", (NODES_PAD, D + H), F32).ap() for L, H in enumerate((4, 4, 8))]
    resid_dram = nc.dram_tensor("resid", (NODES_PAD, D), F32).ap()
    rel_dram = nc.dram_tensor("rel_rows", (STEPS, P), BF16).ap()
    mask_dram = nc.dram_tensor("mask_rows", (8, STEPS, MASKS * P), BF16).ap()
    pass_dram = nc.dram_tensor("pass_rows", (2, STEPS), F32).ap()
    off_dram = nc.dram_tensor("offset_rows", (2, STEPS), I32).ap()

    acc = sbuf(top, "acc", [P, BLOCKS * ACC_W], F32)
    ident = sbuf(top, "ident", [P, P], F32)
    iota_d = sbuf(top, "iota_d", [P, P], F32)
    pidx = sbuf(top, "pidx", [P, 1], F32)
    ones_row = sbuf(top, "ones_row", [1, P], F32)
    rel_col = sbuf(top, "rel_col", [P, STEPS], BF16)
    last_col = sbuf(top, "last_col", [P, STEPS], BF16)
    src_col = sbuf(top, "src_col", [P, STEPS], I32)
    off_row = sbuf(top, "off_row", [2, STEPS + G], I32)
    att = sbuf(top, "att", [P, BLOCKS * 16], F32)
    ad_parts = sbuf(top, "ad_parts", [P, BLOCKS * ADS_W], BF16)
    eps_col = sbuf(top, "eps_col", [P, 1], F32)

    acc3 = acc[:].rearrange("p (b k) -> p b k", k=ACC_W)

    def link_on(engine, s, start=0):
        n = [start]

        def link(ins):
            n[0] += 1
            ins.then_inc(s, 1)
            engine.wait_ge(s, n[0])
        link.n = n
        return link

    s_const, s_in0, s_tile, s_egather, s_p0v = (sem(n) for n in ("s_const", "s_in0", "s_tile", "s_egather", "s_p0v"))
    s_p0t, s_p0c, s_p0o, s_p0off = (sem(n) for n in ("s_p0t", "s_p0c", "s_p0o", "s_p0off"))
    with ExitStack() as ph, nc.Block() as block:
        ends = sbuf(ph, "ends", [P, TILES], F32)
        last_i = acc[:, 0:TILES].bitcast(I32)
        ones_t = sbuf(ph, "ones_t", [P, 1], F32)
        step_no = sbuf(ph, "step_no", [P, SG], F32)
        tile_f = sbuf(ph, "tile_f", [P, SG], F32)
        tile_i = sbuf(ph, "tile_i", [P, SG], I32)
        blk = sbuf(ph, "blk", [P, SG], F32)
        blk128 = sbuf(ph, "blk128", [P, SG], F32)
        offs_f = sbuf(ph, "offs_f", [P, 2 * SG], F32)
        offs_i = sbuf(ph, "offs_i", [P, 2 * SG], I32)
        o = TILES
        edges = acc[:, o:o + SG * 4 * P].bitcast(I32).rearrange("p (j k e) -> p j k e", k=4, e=P)
        o += SG * 4 * P
        rel, valid, first, last, tmp, src_f = (
            acc[:, o + i * STEPS:o + (i + 1) * STEPS].rearrange("p (j e) -> p j e", e=P) for i in range(6))
        o += 6 * STEPS
        masks = sbuf(ph, "masks", [P, SG * MASKS * P], BF16)
        masks4 = masks[:].rearrange("p (j k e) -> p j k e", k=MASKS, e=P)
        relb = sbuf(ph, "relb", [P, STEPS], BF16)
        passes = sbuf(ph, "passes", [P, 2 * SG], F32)
        assert o <= BLOCKS * ACC_W
        ps_c = [psum(ph, f"ps_c{k}", [P, 512]) for k in range(2)]

        @block.gpsimd
        def _(pool):
            nc.gpsimd.memset(ident[:], 0.0).then_inc(s_const, 1)
            pool.wait_ge(s_const, 1)
            nc.gpsimd.affine_select(out=ident[:], in_=ident[:], compare_op=ALU.not_equal, fill=1.0, base=0,
                                    pattern=[[-1, P]], channel_multiplier=1)
            nc.gpsimd.iota(iota_d[:], [[1, P]], 0, 0, allow_small_or_imprecise_dtypes=True)
            nc.gpsimd.iota(pidx[:], [[1, 1]], 0, 1, allow_small_or_imprecise_dtypes=True)
            nc.gpsimd.iota(step_no[:], [[P, SG]], 0, 1, allow_small_or_imprecise_dtypes=True)
            nc.gpsimd.memset(ones_row[:], 1.0)
            nc.gpsimd.memset(eps_col[:], EPS)
            nc.gpsimd.memset(off_row[:], 0)
            nc.gpsimd.memset(ones_t[:], 1.0)
            nc.gpsimd.iota(ends[:], [[1, TILES]], 0, 0, allow_small_or_imprecise_dtypes=True).then_inc(s_const, 1)
            pool.wait_ge(s_tile, 1)
            for j in range(SG):
                pool.indirect_dma_start(edges[:, j, :, :].rearrange("p k e -> p (k e)"), None, t["edge_tiles"],
                                        bass.IndirectOffsetOnAxis(ap=tile_i[:, j:j + 1], axis=0)
                                        ).then_inc(s_egather, 16)

        @block.sync
        def _(sp):
            sp.dma_start(last_i, t["tile_last"][0:1, :].to_broadcast([P, TILES])).then_inc(s_in0, 16)
            sp.wait_ge(s_tile, 2)
            with nc.allow_non_contiguous_dma(reason="a word per partition, once"):
                for k in range(2):
                    sp.dma_start(off_dram[k].rearrange("(j p) -> p j", p=P), offs_i[:, k * SG:(k + 1) * SG]
                                 ).then_inc(s_p0off, 16)
            sp.wait_ge(s_p0off, 32)
            sp.dma_start(off_row[:, 0:STEPS], off_dram[:]).then_inc(s_p0o, 16)
            sp.wait_ge(s_p0c, 1)
            sp.dma_start(rel_dram[:].rearrange("(j p) e -> p j e", p=P),
                         relb[:].rearrange("p (j e) -> p j e", e=P)).then_inc(s_p0o, 16)
            with nc.allow_non_contiguous_dma(reason="a word per partition, once"):
                for k in range(2):
                    sp.dma_start(pass_dram[k].rearrange("(j p) -> p j", p=P), passes[:, k * SG:(k + 1) * SG]
                                 ).then_inc(s_p0o, 16)
            for h in range(8):
                sp.dma_start(mask_dram[h].rearrange("(j p) m -> p j m", p=P),
                             masks[:].rearrange("p (j m) -> p j m", j=SG)).then_inc(s_p0o, 16)
            sp.wait_ge(s_p0o, 16 * 12)

        @block.vector
        def _(dve):
            link = link_on(dve, s_p0v)
            dve.wait_ge(s_in0, 16)
            dve.wait_ge(s_const, 2)
            link(nc.vector.tensor_single_scalar(last_i, last_i, 7, ALU.logical_shift_right))
            link(nc.vector.tensor_tensor(ends[:], ends[:], last_i, ALU.add))
            for j in range(SG):
                link(nc.vector.scalar_tensor_tensor(acc[:, TILES:2 * TILES], ends[:], step_no[:, j:j + 1],
                                                    ones_t[:].to_broadcast([P, TILES]), ALU.is_lt, ALU.mult,
                                                    accum_out=tile_f[:, j:j + 1]))
            link(nc.vector.tensor_scalar(tile_f[:], tile_f[:], float(TILES - 1), None, ALU.min))
            nc.vector.tensor_copy(tile_i[:], tile_f[:]).then_inc(s_tile, 1)
            link(nc.vector.tensor_tensor(blk[:], step_no[:], tile_f[:], ALU.subtract))
            link(nc.vector.tensor_scalar(blk128[:], blk[:], float(P), None, ALU.mult))
            link(nc.vector.tensor_scalar(blk[:], blk[:], float(BLOCKS - 1), None, ALU.min))
            nc.vector.tensor_scalar(offs_f[:, 0:SG], blk[:], float(ACC_W), None, ALU.mult)
            link(nc.vector.tensor_scalar(offs_f[:, SG:], blk[:], float(ADS_W), None, ALU.mult))
            nc.vector.tensor_copy(offs_i[:], offs_f[:]).then_inc(s_tile, 1)
            dve.wait_ge(s_egather, 16 * SG)
            e_src, e_dst, e_prev, e_next = (edges[:, :, k, :] for k in range(4))
            nc.vector.tensor_copy(src_f, e_src)
            link(nc.vector.tensor_tensor(rel, e_dst, blk128[:].unsqueeze(2).to_broadcast([P, SG, P]), ALU.subtract))
            link(nc.vector.tensor_scalar(tmp, rel, 0.0, None, ALU.is_ge))
            link(nc.vector.scalar_tensor_tensor(valid, rel, float(P), tmp, ALU.is_lt, ALU.mult))
            link(nc.vector.scalar_tensor_tensor(rel, rel, 1.0, valid, ALU.add, ALU.mult))
            link(nc.vector.tensor_scalar(rel, rel, -1.0, None, ALU.add))
            nc.vector.tensor_copy(relb[:].rearrange("p (j e) -> p j e", e=P), rel)
            nc.vector.tensor_tensor(first, e_dst, e_prev, ALU.not_equal)
            link(nc.vector.tensor_tensor(last, e_dst, e_next, ALU.not_equal))
            nc.vector.tensor_tensor(first, first, valid, ALU.mult)
            link(nc.vector.tensor_tensor(last, last, valid, ALU.mult))
            nc.vector.tensor_scalar(masks4[:, :, 0, :], valid, -1.0, BIG, ALU.add, ALU.mult)
            nc.vector.tensor_scalar(masks4[:, :, 1, :], first, -BIG, None, ALU.mult)
            link(nc.vector.tensor_scalar(masks4[:, :, 2, :], last, -BIG, None, ALU.mult))
            link(nc.vector.memset(tmp, 0.0))
            for j in range(SG):
                nc.vector.tensor_tensor_scan(masks4[:, j, 3, :], tmp[:, j, :], masks4[:, j, 1, :], 0.0, ALU.add, ALU.min)
                link(nc.vector.tensor_tensor_scan(masks4[:, j, 4, ::-1], tmp[:, j, ::-1], masks4[:, j, 2, ::-1], 0.0,
                                                  ALU.add, ALU.min))
            nc.vector.tensor_copy(passes[:, 0:SG].unsqueeze(2), masks4[:, :, 3, P - 1:P])
            nc.vector.tensor_copy(passes[:, SG:].unsqueeze(2), masks4[:, :, 4, 0:1]).then_inc(s_p0c, 1)
            for j in range(SG):
                dve.wait_ge(s_p0t, j + 1)
                ps = ps_c[j % 2]
                nc.vector.tensor_copy(rel_col[:, j * P:(j + 1) * P], ps[:, 0:P])
                nc.vector.tensor_copy(last_col[:, j * P:(j + 1) * P], ps[:, P:2 * P])
                nc.vector.tensor_copy(src_col[:, j * P:(j + 1) * P], ps[:, 2 * P:3 * P]).then_inc(s_p0c, 1)

        @block.tensor
        def _(pe):
            pe.wait_ge(s_const, 2)
            pe.wait_ge(s_p0c, 1)
            for j in range(SG):
                if j >= 2:
                    pe.wait_ge(s_p0c, j)
                ps = ps_c[j % 2]
                nc.tensor.transpose(ps[:, 0:P], rel[:, j, :], ident[:])
                nc.tensor.transpose(ps[:, P:2 * P], last[:, j, :], ident[:])
                nc.tensor.transpose(ps[:, 2 * P:3 * P], src_f[:, j, :], ident[:]).then_inc(s_p0t, 1)

    if debug == "p0":
        with nc.semaphore("s_dbg") as sd, nc.Block() as block:
            @block.sync
            def _(sp):
                sp.dma_start(t["o_rel"], rel_col[:]).then_inc(sd, 16)
                sp.dma_start(t["o_src"], src_col[:]).then_inc(sd, 16)
                sp.dma_start(t["o_off"], off_row[:, 0:STEPS]).then_inc(sd, 16)
                sp.wait_ge(sd, 48)
        top.close()
        return

    att4 = att[:].rearrange("p (b k h) -> p b k h", k=2, h=8)
    parts4 = ad_parts[:].rearrange("p (b h k) -> p b h k", h=8, k=3)
    HEADS = (4, 4, 8)
    LOOPED = (True, True, False)

    NODE_STAGES = ("w", "prep", "fold", "prep_pe", "prep_act", "chain", "chain_p", "loop_term", "v1", "v2", "v3", "value",
                   "stats", "mean", "root", "rinv", "node", "turned", "xT", "mm", "row", "att", "resid")
    NB = 3
    s = {n: sem("n_" + n) for n in NODE_STAGES}
    s_node, s_loop, s_res, s_st, s_st2 = ([sem(f"n_{n}{k}") for k in range(NB)]
                                          for n in ("node_in", "loop_in", "res_in", "stored", "stored_resid"))

    def clear_node_semaphores():
        with nc.Block() as block:
            @block.gpsimd
            def _(pool):
                for x in [*s.values(), *s_node, *s_loop, *s_res, *s_st, *s_st2]:
                    pool.sem_clear(x)

    def node_phase(before, after):
        tag = f"n{0 if before is None else before + 1}_"
        HB = None if before is None else HEADS[before]
        HA = None if after is None else HEADS[after]
        looped = before is not None and LOOPED[before]
        normed = before in (1, 2)
        linear = after == 2
        with ExitStack() as ph, nc.Block() as block:
            xT = [sbuf(ph, f"{tag}xT{k}", [P, 2, P], F32) for k in range(NB)] if after is not None else None
            node = [sbuf(ph, f"{tag}node{k}", [P, D], F32) for k in range(NB)]
            if before is not None:
                value = [sbuf(ph, f"{tag}value{k}", [P, D], F32) for k in range(NB)]
                share = sbuf(ph, tag + "share", [P, BLOCKS * HB], F32)
                sh3 = share[:].rearrange("p (b h) -> p b h", h=HB)
                calc = [sbuf(ph, f"{tag}calc{k}", [P, BLOCKS * HB], F32) for k in range(4)]
                c3 = [c[:].rearrange("p (b h) -> p b h", h=HB) for c in calc]
            if looped:
                looprow = [sbuf(ph, f"{tag}looprow{k}", [P, D], F32) for k in range(NB)]
                loopterm = [sbuf(ph, f"{tag}loopterm{k}", [P, D], F32) for k in range(NB)]
                own = sbuf(ph, tag + "own", [P, BLOCKS * HB], F32)
                own3 = own[:].rearrange("p (b h) -> p b h", h=HB)
            if normed:
                resrow = [sbuf(ph, f"{tag}resrow{k}", [P, D], F32) for k in range(NB)]
                bias_bc = sbuf(ph, tag + "bias_bc", [P, D], F32)
                stats = [sbuf(ph, f"{tag}stats{k}", [P, 6], F32) for k in range(NB)]
                mv = [sbuf(ph, f"{tag}mv{k}", [P, 2], F32) for k in range(NB)]
                rstd = [sbuf(ph, f"{tag}rstd{k}", [P, 2], F32) for k in range(NB)]
            if before == 0:
                bias_col = sbuf(ph, tag + "bias_col", [P, 2], F32)
            if after is not None:
                WA = D + 2 * HA
                wmat = sbuf(ph, tag + "wmat", [P, 2, WA], F32)
                attb = sbuf(ph, tag + "attb", [P, 2, D], F32)
                prod = sbuf(ph, tag + "prod", [P, 2, D], F32)
                row = [sbuf(ph, f"{tag}row{k}", [P, WA], F32) for k in range(NB)]
                pt = [psum(ph, f"{tag}pt{k}", [P, 512]) for k in range(2)]
                pm = [psum(ph, f"{tag}pm{k}", [P, 512]) for k in range(2)]
                apart = [sbuf(ph, f"{tag}apart{k}", [P, BLOCKS * HA], F32) for k in range(1)]
            if linear:
                wlin = sbuf(ph, tag + "wlin", [P, 2, D], F32)
                wlinT = sbuf(ph, tag + "wlinT", [P, 2, D], F32)
                wall = sbuf(ph, tag + "wall", [P, 2, WA], F32)
                blin_col = sbuf(ph, tag + "blin_col", [P, 2], F32)
                blin_row = sbuf(ph, tag + "blin_row", [1, D], F32)
                ball_row = sbuf(ph, tag + "ball_row", [1, WA], F32)
                resid = [sbuf(ph, f"{tag}resid{k}", [P, D], F32) for k in range(NB)]
                pr = [psum(ph, f"{tag}pr{k}", [P, 512]) for k in range(2)]
                pw = [psum(ph, f"{tag}pw{k}", [P, 512]) for k in range(2)]
            weights = wall if linear else wmat if after is not None else None

            def heads(ap, b, H):
                return ap.rearrange("p (h c) -> p h c", h=H)

            def over(f3, b, H):
                return f3[:, b, :].unsqueeze(2).to_broadcast([P, H, D // H])

            n_w = 0
            def load_constants(q):
                n = 0
                with nc.allow_non_contiguous_dma(reason="a bias in columns, once"):
                    if after is not None:
                        q.dma_start(wmat[:, :, 0:D], t[f"w{after}"].rearrange("(k p) n -> p k n", p=P)).then_inc(s["w"], 16)
                        q.dma_start(attb[:], t[f"att{after}"].rearrange("(o k) n -> o k n", o=1).to_broadcast([P, 2, D])
                                    ).then_inc(s["w"], 16)
                        n += 2
                    if linear:
                        q.dma_start(wlin[:], t["w_lin"].rearrange("(k p) n -> p k n", p=P)).then_inc(s["w"], 16)
                        q.dma_start(blin_col[:], t["b_lin"].rearrange("o (k p) -> p (o k)", p=P)).then_inc(s["w"], 16)
                        q.dma_start(blin_row[:], t["b_lin"]).then_inc(s["w"], 16)
                        n += 3
                    if before == 0:
                        q.dma_start(bias_col[:], t["bias0"].rearrange("o (k p) -> p (o k)", p=P)).then_inc(s["w"], 16)
                        n += 1
                    if normed:
                        q.dma_start(bias_bc[:], t[f"bias{before}"].to_broadcast([P, D])).then_inc(s["w"], 16)
                        n += 1
                return 16 * n
            N_CONST = 16 * ((2 if after is not None else 0) + (3 if linear else 0) + (1 if before in (0, 1, 2) else 0))

            def rows_of(b):
                return slice(b * P, (b + 1) * P)

            def load(q, b):
                if before is None:
                    if b >= NB:
                        q.wait_ge(s["turned"], b - NB + 1)
                    q.dma_start(node[b % NB][:], t["x_pad"][rows_of(b), :]).then_inc(s_node[b % NB], 16)
                if looped:
                    if b >= NB:
                        q.wait_ge(s["loop_term"], b - NB + 1)
                    q.dma_start(looprow[b % NB][:], table[before][rows_of(b), 0:D]).then_inc(s_loop[b % NB], 16)
                if normed:
                    if b >= NB:
                        q.wait_ge(s["loop_term"] if looped else s["value"], b - NB + 1)
                    src = t["x_pad"] if before == 1 else resid_dram
                    q.dma_start(resrow[b % NB][:], src[rows_of(b), :]).then_inc(s_res[b % NB], 16)

            def turn(b):
                return 16 * (b // NB + 1)

            def last_turn(sems):
                return [(sems[k], 16 * len(range(k, BLOCKS, NB))) for k in range(NB)]

            @block.sync
            def _(sp):
                load_constants(sp)
                for b in range(BLOCKS):
                    load(sp, b)

            @block.scalar
            def _(act):
                if before is not None and looped:
                    act.wait_ge(s["prep"], 1)
                    nc.scalar.activation(share[:], calc[0][:], ACT.Exp)
                    nc.scalar.activation(own[:], calc[1][:], ACT.Exp).then_inc(s["prep_act"], 1)

                def root(b):
                    act.wait_ge(s["mean"], b + 1)
                    if b >= NB:
                        act.wait_ge(s["rinv"], b - NB + 1)
                    nc.scalar.activation(rstd[b % NB][:, 0:1], mv[b % NB][:, 1:2], ACT.Sqrt, bias=eps_col[:, 0:1]
                                         ).then_inc(s["root"], 1)

                def x_turned(b):
                    act.wait_ge(s["turned"], b + 1)
                    if b >= NB:
                        act.wait_ge(s["mm"], b - NB + 1)
                    if before == 0:
                        if b == 0:
                            act.wait_ge(s["w"], N_CONST)
                        for k in range(2):
                            last = nc.scalar.activation(xT[b % NB][:, k, :], pt[b % 2][:, k * P:(k + 1) * P], ACT.Relu,
                                                        bias=bias_col[:, k:k + 1])
                    else:
                        last = nc.scalar.copy(xT[b % NB][:].rearrange("p k e -> p (k e)"), pt[b % 2][:, 0:D])
                    last.then_inc(s["xT"], 1)

                def table_row(b):
                    act.wait_ge(s["mm"], b + 1)
                    if b >= NB:
                        act.wait_ge(s_st[b % NB], turn(b - NB))
                        act.wait_ge(s["att"], b - NB + 1)
                    nc.scalar.copy(row[b % NB][:], pm[b % 2][:, 0:WA]).then_inc(s["row"], 1)

                def store_row(b):
                    act.wait_ge(s["row"], b + 1)
                    act.dma_start(table[after][rows_of(b), :], row[b % NB][:, 0:D + HA]).then_inc(s_st[b % NB], 16)

                def store_resid(b):
                    act.wait_ge(s["resid"], b + 1)
                    act.dma_start(resid_dram[rows_of(b), :], resid[b % NB][:]).then_inc(s_st2[b % NB], 16)

                def store_out(b):
                    act.wait_ge(s["node"], b + 1)
                    n = min(P, N_NODES - b * P)
                    act.dma_start(t["out"][b * P:b * P + n, :], node[b % NB][0:n, :]).then_inc(s_st[b % NB], 16)

                steps = []
                if normed:
                    steps.append((1, root))
                if after is not None:
                    steps += [(1, x_turned), (2, table_row), (3, store_row)]
                else:
                    steps.append((3, store_out))
                if linear:
                    steps.append((4, store_resid))
                for i in range(BLOCKS + 5):
                    for lag, step in steps:
                        if 0 <= i - lag < BLOCKS:
                            step(i - lag)
                for q, n in last_turn(s_st) + (last_turn(s_st2) if linear else []):
                    act.wait_ge(q, n)

            @block.gpsimd
            def _(pool):
                if looped:
                    pool.wait_ge(s["prep"], 2)
                    if normed:
                        pool.wait_ge(s["w"], N_CONST)
                    for b in range(BLOCKS):
                        k = b % NB
                        pool.wait_ge(s_loop[k], turn(b))
                        if b >= NB:
                            pool.wait_ge(s["value"], b - NB + 1)
                        ins = nc.gpsimd.tensor_tensor(heads(loopterm[k][:], b, HB), heads(looprow[k][:], b, HB),
                                                      over(own3, b, HB), ALU.mult)
                        if normed:
                            ins.then_inc(s["chain_p"], 1)
                            pool.wait_ge(s_res[k], turn(b))
                            pool.wait_ge(s["chain_p"], b + 1)
                            ins = nc.gpsimd.tensor_tensor(loopterm[k][:], loopterm[k][:], resrow[k][:], ALU.add)
                        ins.then_inc(s["loop_term"], 1)

            @block.vector
            def _(dve):
                link = link_on(dve, s["chain"])
                if before is not None:
                    den, top_a = acc3[:, :, D:D + HB], acc3[:, :, D + HB:D + 2 * HB]
                    a_src, a_dst = att4[:, :, 0, 0:HB], att4[:, :, 1, 0:HB]
                if looped:
                    link(nc.vector.tensor_scalar(c3[0], den, 0.0, -BIG, ALU.is_equal, ALU.mult))
                    link(nc.vector.tensor_tensor(c3[0], c3[0], top_a, ALU.add))
                    link(nc.vector.tensor_tensor(c3[1], c3[0], a_src, ALU.max))
                    link(nc.vector.tensor_tensor(c3[2], c3[0], a_dst, ALU.add))
                    link(nc.vector.tensor_tensor(c3[3], a_src, a_dst, ALU.add))
                    link(nc.vector.tensor_tensor(c3[1], c3[1], a_dst, ALU.add))
                    for c in (1, 2, 3):
                        link(nc.vector.scalar_tensor_tensor(c3[c], c3[c], SLOPE, c3[c], ALU.mult, ALU.max))
                    link(nc.vector.tensor_tensor(c3[0], c3[2], c3[1], ALU.subtract))
                    link(nc.vector.tensor_tensor(c3[1], c3[3], c3[1], ALU.subtract))
                    link(nc.vector.tensor_scalar(c3[0], c3[0], 0.0, None, ALU.min))
                    nc.vector.tensor_scalar(c3[1], c3[1], 0.0, None, ALU.min).then_inc(s["prep"], 1)
                    dve.wait_ge(s["prep_act"], 1)
                    link(nc.vector.tensor_tensor(c3[2], den, sh3, ALU.mult))
                    link(nc.vector.tensor_tensor(c3[2], c3[2], own3, ALU.add))
                    link(nc.vector.tensor_scalar(c3[2], c3[2], 1e-16, None, ALU.max))
                    link(nc.vector.reciprocal(c3[3], c3[2]))
                    link(nc.vector.tensor_tensor(sh3, sh3, c3[3], ALU.mult))
                    nc.vector.tensor_tensor(own3, own3, c3[3], ALU.mult).then_inc(s["prep"], 1)
                    dve.wait_ge(s["prep"], 2)
                elif before is not None:
                    link(nc.vector.scalar_tensor_tensor(c3[0], den, 0.0, den, ALU.is_equal, ALU.add))
                    link(nc.vector.reciprocal(sh3, c3[0]))
                if after is not None:
                    dve.wait_ge(s["w"], N_CONST)
                    C = D // HA
                    for k in range(2):
                        link(nc.vector.tensor_tensor(prod[:], wmat[:, :, 0:D],
                                                     attb[:, k, :].unsqueeze(1).to_broadcast([P, 2, D]), ALU.mult))
                        link(nc.vector.tensor_reduce(wmat[:, :, D + k * HA:D + (k + 1) * HA],
                                                     prod[:].rearrange("p k (h c) -> p k h c", c=C), AX.X, ALU.add))
                if linear:
                    dve.sem_inc(s["prep_pe"], 1)
                    for k in range(2):
                        dve.wait_ge(s["fold"], 1 + k)
                        last = nc.vector.tensor_copy(wlinT[:, k, :], pw[k][:, 0:D])
                    last.then_inc(s["prep_pe"], 1)
                    dve.wait_ge(s["fold"], 3)
                    for k in range(2):
                        last = nc.vector.tensor_copy(wall[:, k, :], pw[k][:, 0:WA])
                    last.then_inc(s["prep_pe"], 1)
                    dve.wait_ge(s["fold"], 4)
                    nc.vector.tensor_copy(ball_row[:], pw[0][0:1, 0:WA]).then_inc(s["prep_pe"], 1)
                elif after is not None:
                    dve.sem_inc(s["prep_pe"], 1)
                if normed:
                    dve.wait_ge(s["w"], N_CONST)

                def value_1(b):
                    k = b % NB
                    if b >= NB:
                        dve.wait_ge(s["node"] if normed else s["turned"], b - NB + 1)
                    num = acc[:, b * ACC_W:b * ACC_W + D]
                    nc.vector.tensor_tensor(heads(value[k][:], b, HB), heads(num, b, HB), over(sh3, b, HB), ALU.mult
                                            ).then_inc(s["v1"], 1)

                def value_2(b):
                    k = b % NB
                    dve.wait_ge(s["v1"], b + 1)
                    if looped:
                        dve.wait_ge(s["loop_term"], b + 1)
                        nc.vector.tensor_tensor(value[k][:], value[k][:], loopterm[k][:], ALU.add).then_inc(s["value" if not normed else "v2"], 1)
                    else:
                        nc.vector.tensor_tensor(value[k][:], value[k][:], bias_bc[:], ALU.add).then_inc(s["v2"], 1)

                def value_3(b):
                    k = b % NB
                    dve.wait_ge(s["v2"], b + 1)
                    if looped:
                        nc.vector.tensor_tensor(value[k][:], value[k][:], bias_bc[:], ALU.add).then_inc(s["value"], 1)
                    else:
                        nc.vector.scalar_tensor_tensor(value[k][:], value[k][:], OUT_SLOPE, value[k][:], ALU.mult, ALU.max
                                                       ).then_inc(s["v3"], 1)

                def value_4(b):
                    k = b % NB
                    dve.wait_ge(s["v3"], b + 1)
                    dve.wait_ge(s_res[k], turn(b))
                    nc.vector.tensor_tensor(value[k][:], value[k][:], resrow[k][:], ALU.add).then_inc(s["value"], 1)

                def statistics(b):
                    dve.wait_ge(s["value"], b + 1)
                    nc.vector.bn_stats(stats[b % NB][:], value[b % NB][:]).then_inc(s["stats"], 1)

                def mean(b):
                    dve.wait_ge(s["stats"], b + 1)
                    nc.vector.bn_aggr(mv[b % NB][:], stats[b % NB][:]).then_inc(s["mean"], 1)

                def rinv(b):
                    dve.wait_ge(s["root"], b + 1)
                    nc.vector.reciprocal(rstd[b % NB][:, 1:2], rstd[b % NB][:, 0:1]).then_inc(s["rinv"], 1)

                def normalise(b):
                    k = b % NB
                    dve.wait_ge(s["rinv"], b + 1)
                    if b >= NB:
                        if after is not None:
                            dve.wait_ge(s["turned"], b - NB + 1)
                            dve.wait_ge(s["resid"], b - NB + 1)
                        else:
                            dve.wait_ge(s_st[k], turn(b - NB))
                    nc.vector.tensor_scalar(node[k][:], value[k][:], mv[k][:, 0:1], rstd[k][:, 1:2], ALU.subtract, ALU.mult
                                            ).then_inc(s["node"], 1)

                def attention(b):
                    dve.wait_ge(s["row"], b + 1)
                    nc.vector.tensor_copy(att4[:, b, :, 0:HA], row[b % NB][:, D:D + 2 * HA].rearrange("p (k h) -> p k h", k=2)
                                          ).then_inc(s["att"], 1)

                def residual(b):
                    k = b % NB
                    dve.wait_ge(s["mm"], b + 1)
                    if b >= NB:
                        dve.wait_ge(s_st2[k], turn(b - NB))
                    nc.vector.tensor_tensor(resid[k][:], node[k][:], pr[b % 2][:, 0:D], ALU.add).then_inc(s["resid"], 1)

                steps = []
                if before is not None:
                    steps += [(0, value_1), (1, value_2)] if not normed else [(0, value_1), (1, value_2), (1, value_3)]
                    if before == 2:
                        steps.append((1, value_4))
                if normed:
                    steps += [(1, statistics), (1, mean), (2, rinv), (2, normalise)]
                if after is not None:
                    steps.append((4, attention))
                if linear:
                    steps.append((4, residual))
                for i in range(BLOCKS + 5):
                    for lag, step in reversed(steps):
                        if 0 <= i - lag < BLOCKS and step in (attention, residual, value_1):
                            step(i - lag)
                    for lag, step in steps:
                        if 0 <= i - lag < BLOCKS and step not in (attention, residual, value_1):
                            step(i - lag)
                if after is not None:
                    dve.wait_ge(s["att"], BLOCKS)
                    ad = att4[:, :, 1, 0:HA]
                    rest = apart[0][:].rearrange("p (b h) -> p b h", h=HA)
                    link(nc.vector.tensor_copy(rest, ad))
                    for k in range(3):
                        link(nc.vector.tensor_copy(parts4[:, :, 0:HA, k], rest))
                        if k < 2:
                            link(nc.vector.tensor_tensor(rest, rest, parts4[:, :, 0:HA, k], ALU.subtract))

            @block.tensor
            def _(pe):
                if after is None:
                    return
                x_now = node if (before is None or normed) else value
                x_ready = (s["node"] if normed else s["value"]) if before is not None else None
                pe.wait_ge(s["prep_pe"], 1)
                if linear:
                    for jc in range(2):
                        for kc in range(2):
                            last = nc.tensor.transpose(pw[jc][:, kc * P:(kc + 1) * P], wlin[:, kc, jc * P:(jc + 1) * P],
                                                       ident[:])
                        last.then_inc(s["fold"], 1)
                    pe.wait_ge(s["prep_pe"], 2)
                    for kc in range(2):
                        for jc in range(2):
                            last = nc.tensor.matmul(pw[kc][:, 0:WA], wlinT[:, jc, kc * P:(kc + 1) * P], wmat[:, jc, :],
                                                    start=(jc == 0), stop=(jc == 1))
                    last.then_inc(s["fold"], 1)
                    pe.wait_ge(s["prep_pe"], 3)
                    for jc in range(2):
                        last = nc.tensor.matmul(pw[0][0:1, 0:WA], blin_col[:, jc:jc + 1], wmat[:, jc, :],
                                                start=(jc == 0), stop=(jc == 1))
                    last.then_inc(s["fold"], 1)
                    pe.wait_ge(s["prep_pe"], 4)

                def turn_block(b):
                    if before is None:
                        pe.wait_ge(s_node[b % NB], turn(b))
                    else:
                        pe.wait_ge(x_ready, b + 1)
                    if b >= 2:
                        pe.wait_ge(s["xT"], b - 1)
                    for k in range(2):
                        last = nc.tensor.transpose(pt[b % 2][:, k * P:(k + 1) * P], x_now[b % NB][:, k * P:(k + 1) * P],
                                                   ident[:])
                    last.then_inc(s["turned"], 1)

                def multiply(b):
                    pe.wait_ge(s["xT"], b + 1)
                    if b >= 2:
                        pe.wait_ge(s["row"], b - 1)
                        if linear:
                            pe.wait_ge(s["resid"], b - 1)
                    if linear:
                        for k in range(2):
                            nc.tensor.matmul(pr[b % 2][:, 0:D], xT[b % NB][:, k, :], wlin[:, k, :], start=(k == 0), stop=False)
                        nc.tensor.matmul(pr[b % 2][:, 0:D], ones_row[:], blin_row[:], start=False, stop=True)
                    for k in range(2):
                        last = nc.tensor.matmul(pm[b % 2][:, 0:WA], xT[b % NB][:, k, :], weights[:, k, :],
                                                start=(k == 0), stop=(k == 1 and not linear))
                    if linear:
                        last = nc.tensor.matmul(pm[b % 2][:, 0:WA], ones_row[:], ball_row[:], start=False, stop=True)
                    last.then_inc(s["mm"], 1)

                for i in range(BLOCKS + 1):
                    if i < BLOCKS:
                        turn_block(i)
                    if i >= 1:
                        multiply(i - 1)

    STAGES = ("compact", "srcT", "onehotT", "onehot", "masked", "scan", "seg", "rowsum", "rowin", "carry", "colsum",
              "tail_sum", "tail", "top1", "top", "topT", "topread", "lookup", "adst", "y1", "l1", "y2", "l2", "dist",
              "gap", "expo", "first_y", "first_l", "first_d", "fdist", "fmat", "factor", "rescaled",
              "msg0", "msg1", "msg2", "msg3", "idx")
    st = {n: sem("e_" + n) for n in STAGES}
    s_mm = [sem(f"e_mm{g}") for g in range(G)]
    s_add = [sem(f"e_add{g}") for g in range(G)]
    s_clear = sem("e_clear")
    s_start = sem("e_start")
    s_apart = sem("e_apart")

    def edge_phase(L):
        H = HEADS[L]
        C = D // H
        HG = H * G
        TW = D + H
        MW = D + 2 * H
        W0 = L * WINDOWS
        N_LOAD = 16 * (4 + H)
        s_gat = [sem(f"e{L}_gathered{k}") for k in range(2)]
        s_ld = [sem(f"e{L}_loaded{k}") for k in range(2)]
        tag = f"e{L}_"
        with ExitStack() as ph, nc.Block() as block:
            rows = [sbuf(ph, f"{tag}rows{k}", [P, G, MW], F32) for k in range(2)]
            idx = [sbuf(ph, f"{tag}idx{k}", [P, G], I32) for k in range(2)]
            onehot = sbuf(ph, tag + "onehot", [P, G, P], F32)
            onehotT = [sbuf(ph, f"{tag}onehotT{k}", [P, G * P], BF16) for k in range(2)]
            mask = [sbuf(ph, f"{tag}mask{k}", [P, MASKS, P], BF16) for k in range(2)]
            passf = [sbuf(ph, f"{tag}passf{k}", [1, H, G], F32) for k in range(2)]
            passb = [sbuf(ph, f"{tag}passb{k}", [1, H, G], F32) for k in range(2)]
            passn = [sbuf(ph, f"{tag}passn{k}", [1, H, 1], F32) for k in range(2)]
            inf, inb, outf, outb = (sbuf(ph, tag + n, [1, H, G], F32) for n in ("inf", "inb", "outf", "outb"))
            nxt = sbuf(ph, tag + "nxt", [1, H, 1], F32)
            tail = sbuf(ph, tag + "tail", [1, H, 1], F32)
            srcc = sbuf(ph, tag + "srcc", [P, H, G], F32)
            srcm, fwd, bwd, seg, top = (sbuf(ph, tag + n, [HG, P], F32) for n in ("srcm", "fwd", "bwd", "seg", "top"))
            adst, y1, l1, y2, l2, dist, gap = (
                sbuf(ph, tag + n, [P, G, H], F32) for n in ("adst", "y1", "l1", "y2", "l2", "dist", "gap"))
            fy, fl, fd, fdiff = (sbuf(ph, tag + n, [1, H], F32) for n in ("fy", "fl", "fd", "fdiff"))
            fcont = sbuf(ph, tag + "fcont", [1, 1], F32)
            factor = sbuf(ph, tag + "factor", [P, H], F32)
            p_mm = [psum(ph, f"{tag}p_mm{k}", [P, 512]) for k in range(4)]
            p_src = psum(ph, tag + "p_src", [P, 512])
            p_look = psum(ph, tag + "p_look", [P, 512])
            p_top = psum(ph, tag + "p_top", [P, 512])
            p_small = psum(ph, tag + "p_small", [P, 512])
            flat = lambda a: a[:].rearrange("o h g -> o (h g)")

            def walk(engine, body):
                def at(w, k, turns, first=False):
                    now = w + (W0 + 1)
                    v = [w, turns, now, now - 1, now - 2]
                    if not isinstance(w, int):
                        v = [engine.snap(x) for x in v]
                    body(v[0], k, v[1], v[2], v[3], v[4], first)
                at(0, 0, 1, True)
                at(1, 1, 1)
                at(2, 0, 2)
                with engine.Fori(1, (WINDOWS - 2) // 2) as i:
                    at(i * 2 + 1, 1, i + 1)
                    at(i * 2 + 2, 0, i + 2)
                at(WINDOWS - 1, 1, WINDOWS // 2)

            def wait(engine, s, n):
                if not (isinstance(n, int) and n <= 0):
                    engine.wait_ge(s, n)

            def wait_apart(engine, s, n):
                if not (isinstance(n, int) and n <= 0):
                    engine.wait_ge(s, n)
                    engine.sem_inc(s_apart, 1)

            def offsets(engine, which, start, n):
                return nc.values_load_multi_w_load_instructions(
                    off_row[which:which + 1, bass.ds(start, n)], engines=[engine.engine], min_val=0,
                    max_val=(BLOCKS - 1) * (ACC_W, ADS_W)[which],
                    skip_runtime_bounds_check_because="phase 0 clamps the block")[1]

            @block.gpsimd
            def _(pool):
                def body(w, k, turns, now, past, past2, first):
                    wait_apart(pool, s_mm[0], past2)
                    nc.gpsimd.tensor_copy(idx[k][:], src_col[:, bass.ds(w * G, G)]).then_inc(st["idx"], 1)
                    wait_apart(pool, st["idx"], now)
                    for g in range(G):
                        if g:
                            wait_apart(pool, s_mm[g], past2)
                        pool.indirect_dma_start(rows[k][:, g, 0:TW], None, table[L],
                                                bass.IndirectOffsetOnAxis(ap=idx[k][:, g:g + 1], axis=0)
                                                ).then_inc(s_gat[k], 16)
                walk(pool, body)

            @block.sync
            def _(sp):
                sp.wait_ge(s_start, L + 1)

                def body(w, k, turns, now, past, past2, first):
                    wait_apart(sp, st["fdist"], past2)
                    wait_apart(sp, st["lookup"], past2)
                    sp.dma_start(onehotT[k][:], rel_dram[bass.ds(w * G, G), :].rearrange("(o g) e -> o (g e)", o=1)
                                 .to_broadcast([P, G * P])).then_inc(s_ld[k], 16)
                    for h in range(H):
                        sp.dma_start(mask[k][h * G:(h + 1) * G, :, :].rearrange("g m e -> g (m e)"),
                                     mask_dram[h, bass.ds(w * G, G), :]).then_inc(s_ld[k], 16)
                    for d, tile, o, n, at in ((0, passf, 1, G - 1, 0), (0, passn, 0, 1, G - 1), (1, passb, 0, G - 1, 1)):
                        sp.dma_start(tile[k][0:1, :, o:o + n], pass_dram[d:d + 1, bass.ds(w * G + at, n)].unsqueeze(1)
                                     .to_broadcast([1, H, n])).then_inc(s_ld[k], 16)
                walk(sp, body)

            @block.scalar
            def _(act):
                def body(w, k, turns, now, past, past2, first):
                    act.wait_ge(s_gat[k], turns * (16 * G))
                    wait(act, st["srcT"], past)
                    nc.scalar.copy(srcc[:], rows[k][:, :, D:D + H].rearrange("p g h -> p h g")).then_inc(st["compact"], 1)
                    act.wait_ge(st["gap"], now)
                    nc.scalar.activation(rows[k][:, :, D:D + H], gap[:], ACT.Exp).then_inc(st["expo"], 1)
                    act.wait_ge(st["fmat"], now)
                    wait(act, st["rescaled"], past)
                    nc.scalar.activation(factor[:], p_small[:, 264:264 + H], ACT.Exp).then_inc(st["factor"], 1)
                walk(act, body)

            @block.tensor
            def _(pe):
                def product(g, k, done, free):
                    if g % 4 == 0:
                        pe.wait_ge(st[f"msg{g // 4}"], done)
                    wait(pe, s_add[(g - 4) % G], free if g < 4 else done)
                    nc.tensor.matmul(p_mm[g % 4][:, 0:MW], onehot[:, g, :], rows[k][:, g, :], start=True, stop=True
                                     ).then_inc(s_mm[g], 1)

                def body(w, k, turns, now, past, past2, first):
                    offs = offsets(pe, 1, w * G, G)
                    def products(a, b):
                        if not first:
                            for g in range(a, b):
                                product(g, 1 - k, past, past2)
                    wait_apart(pe, st["compact"], now)
                    wait_apart(pe, st["masked"], past)
                    nc.tensor.transpose(p_src[0:HG, 0:P], srcc[:].rearrange("p h g -> p (h g)"), ident[:]
                                        ).then_inc(st["srcT"], 1)
                    products(0, 4)
                    pe.wait_ge(st["onehotT"], now)
                    wait(pe, st["adst"], past)
                    for g in range(G):
                        last = nc.tensor.matmul(p_look[:, g * 3 * H:(g + 1) * 3 * H], onehotT[k][:, g * P:(g + 1) * P],
                                                ad_parts[:, bass.ds(offs[g], 3 * H)], start=True, stop=True)
                    last.then_inc(st["lookup"], 1)
                    products(4, 7)
                    wait_apart(pe, st["scan"], now)
                    wait_apart(pe, st["factor"], past)
                    for dst, col, o in ((0, fwd[:, P - 1:P], 0), (1, bwd[:, 0:1], P)):
                        last = nc.tensor.matmul(p_small[0:1, o:o + HG], col, ident[0:HG, 0:HG], start=True, stop=True)
                    last.then_inc(st["rowsum"], 1)
                    products(7, 9)
                    wait_apart(pe, st["carry"], now)
                    for o, src in ((256, outf), (257, outb)):
                        last = nc.tensor.matmul(p_small[0:HG, o:o + 1], flat(src), ones_row[0:1, 0:1],
                                                start=True, stop=True)
                    last.then_inc(st["colsum"], 1)
                    products(9, 11)
                    wait_apart(pe, st["top"], now)
                    wait_apart(pe, st["topread"], past)
                    nc.tensor.transpose(p_top[:, 0:HG], top[:], ident[0:HG, 0:HG]).then_inc(st["topT"], 1)
                    products(11, 16)
                    wait_apart(pe, st["fdist"], now)
                    nc.tensor.matmul(p_small[:, 264:264 + H], onehot[0:1, 0, :], fdiff[:], start=True, stop=True
                                     ).then_inc(st["fmat"], 1)
                walk(pe, body)
                for g in range(G):
                    product(g, 1, W0 + WINDOWS, W0 + WINDOWS - 1)

            @block.vector
            def _(dve):
                def add(g, off, done):
                    dve.wait_ge(s_mm[g], done)
                    wait(dve, s_add[g - 1] if g else st["rescaled"], done)
                    sums = acc[:, bass.ds(off, MW)]
                    nc.vector.tensor_tensor(sums, sums, p_mm[g % 4][:, 0:MW], ALU.add).then_inc(s_add[g], 1)

                def body(w, k, turns, now, past, past2, first):
                    offs = offsets(dve, 0, 0, 1) if first else offsets(dve, 0, (w - 1) * G, G + 1)
                    m = mask[k]

                    def adds(*gs):
                        for g in gs:
                            if not first:
                                add(g, offs[g], past)

                    def one_hot(q):
                        rel = rel_col[:, bass.ds(w * G + 4 * q, 4)]
                        nc.vector.tensor_tensor(onehot[:, 4 * q:4 * q + 4, :], rel.unsqueeze(2).to_broadcast([P, 4, P]),
                                                iota_d[:].unsqueeze(1).to_broadcast([P, 4, P]), ALU.is_equal)

                    dve.wait_ge(s_ld[k], turns * N_LOAD)
                    dve.wait_ge(st["srcT"], now)
                    nc.vector.tensor_tensor(srcm[:], p_src[0:HG, 0:P], m[0:HG, 0, :], ALU.add).then_inc(st["masked"], 1)
                    adds(0)
                    nc.vector.tensor_scalar(onehotT[k][:], onehotT[k][:], pidx[:, 0:1], None, ALU.is_equal
                                            ).then_inc(st["onehotT"], 1)
                    dve.wait_ge(st["masked"], now)
                    nc.vector.tensor_tensor_scan(fwd[:], m[0:HG, 1, :], srcm[:], -BIG, ALU.add, ALU.max)
                    nc.vector.tensor_tensor_scan(bwd[:, ::-1], m[0:HG, 2, ::-1], srcm[:, ::-1], -BIG, ALU.add, ALU.max
                                                 ).then_inc(st["scan"], 1)
                    adds(1, 2)
                    dve.wait_ge(st["scan"], now)
                    nc.vector.tensor_tensor(seg[:], fwd[:], bwd[:], ALU.max).then_inc(st["seg"], 1)
                    dve.wait_ge(st["rowsum"], now)
                    rf = p_small[0:1, 0:HG].rearrange("o (h g) -> o h g", g=G)
                    rb = p_small[0:1, P:P + HG].rearrange("o (h g) -> o h g", g=G)
                    if first:
                        nc.vector.memset(inf[:, :, 0:1], -BIG)
                    else:
                        nc.vector.tensor_copy(inf[:, :, 0:1], nxt[:])
                    nc.vector.tensor_copy(inf[:, :, 1:G], rf[:, :, 0:G - 1])
                    nc.vector.tensor_copy(tail[:], rf[:, :, G - 1:G])
                    nc.vector.tensor_copy(inb[:, :, 0:G - 1], rb[:, :, 1:G]).then_inc(st["rowin"], 1)
                    adds(3)
                    one_hot(0)
                    dve.wait_ge(st["rowin"], now)
                    nc.vector.tensor_tensor_scan(flat(outf), flat(passf[k]), flat(inf), -BIG, ALU.add, ALU.max)
                    nc.vector.tensor_tensor_scan(flat(outb)[:, ::-1], flat(passb[k])[:, ::-1], flat(inb)[:, ::-1], -BIG,
                                                 ALU.add, ALU.max).then_inc(st["carry"], 1)
                    adds(4)
                    dve.wait_ge(st["carry"], now)
                    nc.vector.tensor_tensor(nxt[:], outf[:, :, G - 1:G], passn[k][:], ALU.add).then_inc(st["tail_sum"], 1)
                    adds(5)
                    dve.wait_ge(st["tail_sum"], now)
                    nc.vector.tensor_tensor(nxt[:], nxt[:], tail[:], ALU.max).then_inc(st["tail"], 1)
                    dve.wait_ge(st["lookup"], now)
                    nc.vector.tensor_reduce(adst[:].rearrange("p g h -> p (g h)"),
                                            p_look[:, 0:3 * HG].rearrange("p (n k) -> p n k", k=3), AX.X, ALU.add
                                            ).then_inc(st["adst"], 1)
                    adds(6)
                    dve.wait_ge(st["adst"], now)
                    nc.vector.tensor_tensor(y1[:], rows[k][:, :, D:D + H], adst[:], ALU.add).then_inc(st["y1"], 1)
                    dve.wait_ge(st["colsum"], now)
                    nc.vector.scalar_tensor_tensor(top[:], m[0:HG, 3, :], p_small[0:HG, 256:257], seg[:], ALU.add, ALU.max
                                                   ).then_inc(st["top1"], 1)
                    adds(7)
                    one_hot(1)
                    dve.wait_ge(st["top1"], now)
                    nc.vector.scalar_tensor_tensor(top[:], m[0:HG, 4, :], p_small[0:HG, 257:258], top[:], ALU.add, ALU.max
                                                   ).then_inc(st["top"], 1)
                    dve.wait_ge(st["y1"], now)
                    nc.vector.scalar_tensor_tensor(l1[:], y1[:], SLOPE, y1[:], ALU.mult, ALU.max).then_inc(st["l1"], 1)
                    adds(8, 9)
                    dve.wait_ge(st["topT"], now)
                    top_e = p_top[:, 0:HG].rearrange("p (h g) -> p g h", g=G)
                    nc.vector.tensor_tensor(y2[:], top_e, adst[:], ALU.add).then_inc(st["y2"], 1)
                    nc.vector.tensor_tensor(rows[k][:, :, D + H:MW], top_e,
                                            last_col[:, bass.ds(w * G, G)].unsqueeze(2).to_broadcast([P, G, H]), ALU.mult
                                            ).then_inc(st["topread"], 1)
                    adds(10)
                    dve.wait_ge(st["y2"], now)
                    nc.vector.scalar_tensor_tensor(l2[:], y2[:], SLOPE, y2[:], ALU.mult, ALU.max).then_inc(st["l2"], 1)
                    adds(11)
                    one_hot(2)
                    dve.wait_ge(st["l2"], now)
                    nc.vector.tensor_tensor(dist[:], l1[:], l2[:], ALU.subtract).then_inc(st["dist"], 1)
                    nc.vector.tensor_tensor(fy[:], inf[:, :, 0], adst[0:1, 0, :], ALU.add).then_inc(st["first_y"], 1)
                    nc.vector.tensor_tensor(fcont[:], m[0:1, 0, 0:1], m[0:1, 1, 0:1], ALU.add)
                    adds(12)
                    dve.wait_ge(st["dist"], now)
                    nc.vector.tensor_scalar(gap[:], dist[:], 0.0, None, ALU.min).then_inc(st["gap"], 1)
                    dve.wait_ge(st["first_y"], now)
                    nc.vector.scalar_tensor_tensor(fl[:], fy[:], SLOPE, fy[:], ALU.mult, ALU.max).then_inc(st["first_l"], 1)
                    adds(13)
                    dve.wait_ge(st["first_l"], now)
                    nc.vector.tensor_tensor(fd[:], fl[:], l2[0:1, 0, :], ALU.subtract).then_inc(st["first_d"], 1)
                    adds(14)
                    dve.wait_ge(st["first_d"], now)
                    nc.vector.scalar_tensor_tensor(fdiff[:], fcont[:].to_broadcast([1, H]), -1.0, fd[:], ALU.is_ge, ALU.mult
                                                   ).then_inc(st["fdist"], 1)
                    adds(15)
                    one_hot(3)
                    dve.wait_ge(st["expo"], now)
                    for q in range(4):
                        g4 = slice(4 * q, 4 * q + 4)
                        feats = rows[k][:, g4, 0:D].rearrange("p g (h c) -> p g h c", h=H)
                        nc.vector.tensor_tensor(feats, feats, rows[k][:, g4, D:D + H].unsqueeze(3).to_broadcast([P, 4, H, C]),
                                                ALU.mult).then_inc(st[f"msg{q}"], 1)
                    dve.wait_ge(st["factor"], now)
                    wait(dve, s_add[G - 1], past)
                    off = offs[-1]
                    num = acc[:, bass.ds(off, D)].rearrange("p (h c) -> p h c", h=H)
                    nc.vector.tensor_tensor(num, num, factor[:].unsqueeze(2).to_broadcast([P, H, C]), ALU.mult)
                    den = acc[:, bass.ds(off + D, H)]
                    nc.vector.tensor_tensor(den, den, factor[:], ALU.mult).then_inc(st["rescaled"], 1)

                nc.vector.memset(inb[:], -BIG)
                for tile in (*passf, *passb):
                    last = nc.vector.memset(tile[:], -BIG)
                last.then_inc(s_start, 1)
                nc.vector.memset(acc[:], 0.0).then_inc(s_clear, 1)
                dve.wait_ge(s_clear, L + 1)
                walk(dve, body)
                offs = offsets(dve, 0, (WINDOWS - 1) * G, G)
                for g in range(G):
                    add(g, offs[g], W0 + WINDOWS)

    node_phase(None, 0)
    if debug == "n0":
        top.close()
        return
    for L in range(3):
        edge_phase(L)
        clear_node_semaphores()
        node_phase(L, L + 1 if L < 2 else None)
    top.close()


def kernel(x, src, dst, L0_gnn_W1, L0_gnn_att_src1, L0_gnn_att_dst1, L0_gnn_b1, L0_gnn_W2, L0_gnn_att_src2,
           L0_gnn_att_dst2, L0_gnn_b2, L1_gnn_W_lin, L1_gnn_b_lin, L1_gnn_W_gat, L1_gnn_attn_l, L1_gnn_attn_r,
           L1_gnn_gat_bias):
    import numpy as np
    import concourse.bacc as bacc
    from concourse.bass_utils import run_bass_kernel_spmd

    def flat_row(a):
        return np.ascontiguousarray(np.asarray(a).reshape(1, -1))

    x = np.asarray(x)
    x_pad = np.zeros((NODES_PAD, D), x.dtype)
    x_pad[:N_NODES] = x
    src, dst = (np.asarray(a) for a in (src, dst))
    src_pad = np.zeros(EDGES_PAD, src.dtype)
    src_pad[:N_EDGES] = src
    dst_pad = np.full(EDGES_PAD + 2, -1, dst.dtype)
    dst_pad[1:-1] = NODES_PAD - 1
    dst_pad[1:N_EDGES + 1] = dst
    edge_tiles = np.concatenate([a.reshape(TILES, P) for a in (src_pad, dst_pad[1:-1], dst_pad[:-2], dst_pad[2:])], axis=1)
    tile_last = np.ascontiguousarray(dst_pad[1:-1].reshape(TILES, P)[:, -1])[None]
    arrays = {
        "x_pad": x_pad, "edge_tiles": edge_tiles, "tile_last": tile_last,
        "w0": np.asarray(L0_gnn_W1), "w1": np.asarray(L0_gnn_W2), "w2": np.asarray(L1_gnn_W_gat),
        "w_lin": np.asarray(L1_gnn_W_lin), "b_lin": flat_row(L1_gnn_b_lin),
        "att0": np.concatenate([flat_row(L0_gnn_att_src1), flat_row(L0_gnn_att_dst1)]),
        "att1": np.concatenate([flat_row(L0_gnn_att_src2), flat_row(L0_gnn_att_dst2)]),
        "att2": np.concatenate([flat_row(L1_gnn_attn_l), flat_row(L1_gnn_attn_r)]),
        "bias0": flat_row(L0_gnn_b1), "bias1": flat_row(L0_gnn_b2), "bias2": flat_row(L1_gnn_gat_bias),
    }
    nc = bacc.Bacc("TRN2", target_bir_lowering=False, num_devices=1)
    t = {n: nc.dram_tensor(f"in_{n}", a.shape, mybir.dt.from_np(a.dtype), kind="ExternalInput").ap()
         for n, a in arrays.items()}
    t["out"] = nc.dram_tensor("result", (N_NODES, D), F32, kind="ExternalOutput").ap()
    build_program(nc, t)
    r = run_bass_kernel_spmd(nc, [{f"in_{n}": a for n, a in arrays.items()}], core_ids=[0])
    return r.results[0]["result"]
```

```python
import concourse.bass as bass
from concourse import mybir
from contextlib import ExitStack

F32 = mybir.dt.float32
BF16 = mybir.dt.bfloat16
I32 = mybir.dt.int32
ALU = mybir.AluOpType
ACT = mybir.ActivationFunctionType
AX = mybir.AxisListType
ENG = mybir.EngineType

P = 128
N_NODES = 12500
N_EDGES = 200000
D = 256
TILES = -(-N_EDGES // P)
BLOCKS = -(-N_NODES // P)
NODES_PAD = BLOCKS * P
EDGES_PAD = TILES * P
G = 16
WINDOWS = -(-(TILES + BLOCKS - 1) // G)
WINDOWS = -(-WINDOWS // (P // G)) * (P // G)
STEPS = WINDOWS * G
SG = STEPS // P
assert STEPS == SG * P
ACC_W = D + 16
ADS_W = 24
MASKS = 5
BUFS = 3
REGIONS = 4
BANK = 512
WIN = 8
TABLES_FIRST, TABLES_COLUMNS = 28, 66
BIG = 1e30
SLOPE = 0.2
OUT_SLOPE = 0.01
EPS = 1e-5


def build_program(nc, t):
    top = ExitStack()

    def sbuf(stack, name, shape, dtype):
        return stack.enter_context(nc.sbuf_tensor(name, shape, dtype))

    def psum(stack, name, shape, dtype=F32):
        return stack.enter_context(nc.psum_tensor(name, shape, dtype))

    def sem(name):
        return top.enter_context(nc.semaphore(name))

    table = [nc.dram_tensor(f"table{L}", (NODES_PAD, D + H), F32).ap() for L, H in enumerate((4, 4, 8))]
    resid_dram = nc.dram_tensor("resid", (NODES_PAD, D), F32).ap()
    rel_dram = nc.dram_tensor("rel_rows", (STEPS, P), BF16).ap()
    mask_dram = nc.dram_tensor("mask_rows", (STEPS, MASKS * P), BF16).ap()
    src_dram = nc.dram_tensor("src_cols", (WINDOWS, P, G), I32).ap()
    col_dram = nc.dram_tensor("edge_cols", (WINDOWS, P, 2, G), BF16).ap()
    pass_dram = nc.dram_tensor("pass_rows", (2, STEPS), F32).ap()
    off_dram = nc.dram_tensor("offset_rows", (3, STEPS), I32).ap()
    win_dram = nc.dram_tensor("window_rows", (WINDOWS, WIN), I32).ap()

    acc = sbuf(top, "acc", [P, BLOCKS * ACC_W], F32)
    ident = sbuf(top, "ident", [P, P], F32)
    iota_d = sbuf(top, "iota_d", [P, P], F32)
    pidx = sbuf(top, "pidx", [P, 1], F32)
    ones_row = sbuf(top, "ones_row", [1, P], F32)
    beyond_d = sbuf(top, "beyond_d", [P, P], F32)
    zeros = sbuf(top, "zeros", [1, ACC_W], BF16)
    off_row = sbuf(top, "off_row", [4, STEPS], I32)
    as32 = sbuf(top, "as32", [P, BLOCKS * 8], F32)
    ad_parts = sbuf(top, "ad_parts", [P, BLOCKS * ADS_W], BF16)
    eps_col = sbuf(top, "eps_col", [P, 1], F32)

    acc3 = acc[:].rearrange("p (b k) -> p b k", k=ACC_W)

    def link_on(engine, s, start=0):
        n = [start]

        def link(ins):
            n[0] += 1
            ins.then_inc(s, 1)
            engine.wait_ge(s, n[0])
        link.n = n
        return link

    s_const, s_in0, s_tile, s_egather, s_p0v = (sem(n) for n in ("s_const", "s_in0", "s_tile", "s_egather", "s_p0v"))
    s_p0t, s_p0c, s_p0o, s_p0off = (sem(n) for n in ("s_p0t", "s_p0c", "s_p0o", "s_p0off"))
    s_p0win, s_p0pick, s_p0blk0 = (sem(n) for n in ("s_p0win", "s_p0pick", "s_p0blk0"))

    def step_tables(ph):
        ends = sbuf(ph, "ends", [P, TILES], F32)
        last_i = acc[:, 0:TILES].bitcast(I32)
        ones_t = sbuf(ph, "ones_t", [P, 1], F32)
        step_no = sbuf(ph, "step_no", [P, SG], F32)
        tile_f = sbuf(ph, "tile_f", [P, SG], F32)
        tile_i = sbuf(ph, "tile_i", [P, SG], I32)
        blk = sbuf(ph, "blk", [P, SG], F32)
        blk128 = sbuf(ph, "blk128", [P, SG], F32)
        blk0, into, sign = (sbuf(ph, n, [P, SG], F32) for n in ("blk0", "into", "sign"))
        pick = sbuf(ph, "pick", [P, P], F32)
        offs_f = sbuf(ph, "offs_f", [P, 3 * SG], F32)
        offs_i = sbuf(ph, "offs_i", [P, 3 * SG], I32)
        win_f = sbuf(ph, "win_f", [P, SG, WIN], F32)
        win_i = sbuf(ph, "win_i", [P, SG, WIN], I32)
        src_col = sbuf(ph, "src_col", [P, STEPS], I32)
        cols = sbuf(ph, "cols", [P, 2, STEPS], BF16)
        o = TILES
        edges = acc[:, o:o + SG * 4 * P].bitcast(I32).rearrange("p (j k e) -> p j k e", k=4, e=P)
        o += SG * 4 * P
        rel, valid, first, last, tmp, src_f, rel_c = (
            acc[:, o + i * STEPS:o + (i + 1) * STEPS].rearrange("p (j e) -> p j e", e=P) for i in range(7))
        o += 7 * STEPS
        masks = sbuf(ph, "masks", [P, SG * MASKS * P], BF16)
        masks4 = masks[:].rearrange("p (j k e) -> p j k e", k=MASKS, e=P)
        relb = sbuf(ph, "relb", [P, STEPS], BF16)
        passes = sbuf(ph, "passes", [P, 2 * SG], F32)
        assert o <= BLOCKS * ACC_W
        ps_c = [psum(ph, f"ps_c{k}", [P, 512]) for k in range(2)]

        def start(sp):
            sp.dma_start(last_i, t["tile_last"][0:1, :].to_broadcast([P, TILES])).then_inc(s_in0, 16)

        def on_pool(pool):
            nc.gpsimd.memset(ident[:], 0.0).then_inc(s_const, 1)
            pool.wait_ge(s_const, 1)
            nc.gpsimd.affine_select(out=ident[:], in_=ident[:], compare_op=ALU.not_equal, fill=1.0, base=0,
                                    pattern=[[-1, P]], channel_multiplier=1)
            nc.gpsimd.iota(iota_d[:], [[1, P]], 0, 0, allow_small_or_imprecise_dtypes=True)
            nc.gpsimd.iota(pidx[:], [[1, 1]], 0, 1, allow_small_or_imprecise_dtypes=True)
            nc.gpsimd.iota(step_no[:], [[P, SG]], 0, 1, allow_small_or_imprecise_dtypes=True)
            nc.gpsimd.memset(ones_row[:], 1.0)
            nc.gpsimd.memset(eps_col[:], EPS)
            nc.gpsimd.iota(beyond_d[:], [[-1, P]], -2, 0, allow_small_or_imprecise_dtypes=True)
            nc.gpsimd.iota(pick[:], [[G, P // G], [0, G]], 0, -1, allow_small_or_imprecise_dtypes=True)
            nc.gpsimd.memset(zeros[:], 0.0)
            nc.gpsimd.memset(off_row[:], 0)
            nc.gpsimd.memset(ones_t[:], 1.0)
            nc.gpsimd.iota(ends[:], [[1, TILES]], 0, 0, allow_small_or_imprecise_dtypes=True).then_inc(s_const, 1)
            pool.wait_ge(s_tile, 1)
            for j in range(SG):
                pool.indirect_dma_start(edges[:, j, :, :].rearrange("p k e -> p (k e)"), None, t["edge_tiles"],
                                        bass.IndirectOffsetOnAxis(ap=tile_i[:, j:j + 1], axis=0)
                                        ).then_inc(s_egather, 16)
            pool.wait_ge(s_tile, 2)
            with nc.allow_non_contiguous_dma(reason="a word per partition, once"):
                for k in range(3):
                    pool.dma_start(off_dram[k].rearrange("(j p) -> p j", p=P), offs_i[:, k * SG:(k + 1) * SG]
                                 ).then_inc(s_p0off, 16)
            pool.wait_ge(s_p0off, 48)
            pool.dma_start(off_row[0:3, :], off_dram[:]).then_inc(s_p0o, 16)
            with nc.allow_non_contiguous_dma(reason="a few words per window, once"):
                by_group = win_dram[:].rearrange("(j w) c -> w j c", w=P // G)
                pool.dma_start(by_group[:, :, 0:REGIONS], win_i[0:P:G, :, 0:REGIONS]).then_inc(s_p0win, 16)
                pool.dma_start(by_group[:, :, REGIONS:WIN], win_i[G - 1:P:G, :, REGIONS:WIN]).then_inc(s_p0win, 16)
            pool.wait_ge(s_p0win, 32)
            pool.dma_start(off_row[3:4, 0:WINDOWS * WIN], win_dram[:].rearrange("(o w) c -> o (w c)", o=1)
                         ).then_inc(s_p0o, 16)
            pool.wait_ge(s_p0c, 1)
            pool.dma_start(rel_dram[:].rearrange("(j p) e -> p j e", p=P),
                         relb[:].rearrange("p (j e) -> p j e", e=P)).then_inc(s_p0o, 16)
            with nc.allow_non_contiguous_dma(reason="a word per partition, once"):
                for k in range(2):
                    pool.dma_start(pass_dram[k].rearrange("(j p) -> p j", p=P), passes[:, k * SG:(k + 1) * SG]
                                 ).then_inc(s_p0o, 16)
            pool.dma_start(mask_dram[:].rearrange("(j p) m -> p j m", p=P),
                           masks[:].rearrange("p (j m) -> p j m", j=SG)).then_inc(s_p0o, 16)
            pool.wait_ge(s_p0c, 1 + SG)
            pool.dma_start(src_dram[:].rearrange("w p g -> p w g"), src_col[:].rearrange("p (w g) -> p w g", g=G)
                         ).then_inc(s_p0o, 16)
            for k in range(2):
                pool.dma_start(col_dram[:, :, k, :].rearrange("w p g -> p w g"),
                             cols[:, k, :].rearrange("p (w g) -> p w g", g=G)).then_inc(s_p0o, 16)
            pool.wait_ge(s_p0o, 9 * 16)

        def on_dve(dve):
            link = link_on(dve, s_p0v)
            dve.wait_ge(s_in0, 16)
            dve.wait_ge(s_const, 2)
            link(nc.vector.tensor_single_scalar(last_i, last_i, 7, ALU.logical_shift_right))
            link(nc.vector.tensor_tensor(ends[:], ends[:], last_i, ALU.add))
            for j in range(SG):
                link(nc.vector.scalar_tensor_tensor(acc[:, TILES:2 * TILES], ends[:], step_no[:, j:j + 1],
                                                    ones_t[:].to_broadcast([P, TILES]), ALU.is_lt, ALU.mult,
                                                    accum_out=tile_f[:, j:j + 1]))
            link(nc.vector.tensor_scalar(tile_f[:], tile_f[:], float(TILES - 1), None, ALU.min))
            nc.vector.tensor_copy(tile_i[:], tile_f[:]).then_inc(s_tile, 1)
            link(nc.vector.tensor_tensor(blk[:], step_no[:], tile_f[:], ALU.subtract))
            link(nc.vector.tensor_scalar(blk128[:], blk[:], float(P), None, ALU.mult))
            link(nc.vector.tensor_scalar(blk[:], blk[:], float(BLOCKS - 1), None, ALU.min))
            nc.vector.tensor_scalar(pick[:], pick[:], 0.0, None, ALU.is_equal).then_inc(s_p0pick, 1)
            dve.wait_ge(s_p0blk0, 1)
            link(nc.vector.tensor_copy(blk0[:], ps_c[0][:, 0:SG]))
            link(nc.vector.tensor_tensor(into[:], blk[:], blk0[:], ALU.subtract))
            link(nc.vector.tensor_scalar(offs_f[:, 0:SG], into[:], float(REGIONS - 1), float(BANK), ALU.min, ALU.mult))
            link(nc.vector.tensor_scalar(offs_f[:, SG:2 * SG], blk[:], float(ADS_W), None, ALU.mult))
            link(nc.vector.tensor_scalar(offs_f[:, 2 * SG:], blk[:], float(ACC_W), None, ALU.mult))
            link(nc.vector.tensor_scalar(sign[:], into[:], float(REGIONS), -2.0, ALU.is_ge, ALU.mult))
            link(nc.vector.tensor_scalar(sign[:], sign[:], 1.0, None, ALU.add))
            link(nc.vector.memset(win_f[:], 0.0))
            for r in range(REGIONS):
                link(nc.vector.tensor_scalar(win_f[:, :, r], blk0[:], float(BLOCKS - r), float(-REGIONS), ALU.is_ge,
                                             ALU.mult))
                link(nc.vector.scalar_tensor_tensor(win_f[:, :, r], blk0[:], float(r), win_f[:, :, r], ALU.add, ALU.add))
                link(nc.vector.tensor_scalar(win_f[:, :, r], win_f[:, :, r], float(ACC_W), None, ALU.mult))
            link(nc.vector.tensor_scalar(win_f[:, :, REGIONS], into[:], float(REGIONS), None, ALU.is_ge))
            nc.vector.tensor_copy(offs_i[:], offs_f[:])
            nc.vector.tensor_copy(win_i[:], win_f[:]).then_inc(s_tile, 1)
            dve.wait_ge(s_egather, 16 * SG)
            e_src, e_dst, e_prev, e_next = (edges[:, :, k, :] for k in range(4))
            nc.vector.tensor_copy(src_f, e_src)
            link(nc.vector.tensor_tensor(rel, e_dst, blk128[:].unsqueeze(2).to_broadcast([P, SG, P]), ALU.subtract))
            link(nc.vector.tensor_scalar(tmp, rel, 0.0, None, ALU.is_ge))
            link(nc.vector.scalar_tensor_tensor(valid, rel, float(P), tmp, ALU.is_lt, ALU.mult))
            link(nc.vector.scalar_tensor_tensor(rel, rel, 1.0, valid, ALU.add, ALU.mult))
            link(nc.vector.tensor_tensor(rel_c, rel, sign[:].unsqueeze(2).to_broadcast([P, SG, P]), ALU.mult))
            link(nc.vector.tensor_scalar(rel_c, rel_c, -1.0, None, ALU.add))
            link(nc.vector.tensor_scalar(rel, rel, -1.0, None, ALU.add))
            nc.vector.tensor_copy(relb[:].rearrange("p (j e) -> p j e", e=P), rel)
            nc.vector.tensor_tensor(first, e_dst, e_prev, ALU.not_equal)
            link(nc.vector.tensor_tensor(last, e_dst, e_next, ALU.not_equal))
            nc.vector.tensor_tensor(first, first, valid, ALU.mult)
            link(nc.vector.tensor_tensor(last, last, valid, ALU.mult))
            nc.vector.tensor_scalar(masks4[:, :, 0, :], valid, -1.0, BIG, ALU.add, ALU.mult)
            nc.vector.tensor_scalar(masks4[:, :, 1, :], first, -BIG, None, ALU.mult)
            link(nc.vector.tensor_scalar(masks4[:, :, 2, :], last, -BIG, None, ALU.mult))
            link(nc.vector.memset(tmp, 0.0))
            for j in range(SG):
                nc.vector.tensor_tensor_scan(masks4[:, j, 3, :], tmp[:, j, :], masks4[:, j, 1, :], 0.0, ALU.add, ALU.min)
                link(nc.vector.tensor_tensor_scan(masks4[:, j, 4, ::-1], tmp[:, j, ::-1], masks4[:, j, 2, ::-1], 0.0,
                                                  ALU.add, ALU.min))
            nc.vector.tensor_copy(passes[:, 0:SG].unsqueeze(2), masks4[:, :, 3, P - 1:P])
            nc.vector.tensor_copy(passes[:, SG:].unsqueeze(2), masks4[:, :, 4, 0:1]).then_inc(s_p0c, 1)
            for j in range(SG):
                dve.wait_ge(s_p0t, j + 1)
                ps = ps_c[j % 2]
                nc.vector.tensor_copy(cols[:, 0, j * P:(j + 1) * P], ps[:, 0:P])
                nc.vector.tensor_copy(cols[:, 1, j * P:(j + 1) * P], ps[:, P:2 * P])
                nc.vector.tensor_copy(src_col[:, j * P:(j + 1) * P], ps[:, 2 * P:3 * P]).then_inc(s_p0c, 1)

        def first_blocks(pe):
            pe.wait_ge(s_p0pick, 1)
            nc.tensor.matmul(ps_c[0][:, 0:SG], pick[:], blk[:], start=True, stop=True).then_inc(s_p0blk0, 1)

        def columns(pe):
            pe.wait_ge(s_p0c, 1)
            for j in range(SG):
                if j >= 2:
                    pe.wait_ge(s_p0c, j)
                ps = ps_c[j % 2]
                nc.tensor.transpose(ps[:, 0:P], rel_c[:, j, :], ident[:])
                nc.tensor.transpose(ps[:, P:2 * P], last[:, j, :], ident[:])
                nc.tensor.transpose(ps[:, 2 * P:3 * P], src_f[:, j, :], ident[:]).then_inc(s_p0t, 1)

        return start, on_pool, on_dve, first_blocks, columns

    as3 = as32[:].rearrange("p (b h) -> p b h", h=8)
    parts4 = ad_parts[:].rearrange("p (b h k) -> p b h k", h=8, k=3)
    HEADS = (4, 4, 8)
    LOOPED = (True, True, False)

    NODE_STAGES = ("w", "prep", "fold", "prep_pe", "prep_act", "chain", "chain_p", "loop_term", "v1", "v2", "v3", "value",
                   "stats", "mean", "root", "rinv", "shift", "node", "turned", "xT", "mm", "row", "att", "resid")
    DEPTH = {"node": 8, "value": 14, "looprow": 3, "loopterm": 4, "resrow": 5, "xT": 3, "row": 5, "resid": 5}
    s = {n: sem("n_" + n) for n in NODE_STAGES}
    s_node, s_loop, s_res, s_row, s_out, s_rst = (
        [sem(f"n_dma_{n}{k}") for k in range(DEPTH[n.split("_")[0]])]
        for n in ("node", "looprow", "resrow", "row", "node_out", "resid"))

    def clear_node_semaphores():
        with nc.Block() as block:
            @block.gpsimd
            def _(pool):
                for x in [*s.values(), *s_node, *s_loop, *s_res, *s_row, *s_out, *s_rst]:
                    pool.sem_clear(x)

    def node_phase(before, after):
        tag = f"n{0 if before is None else before + 1}_"
        HB = None if before is None else HEADS[before]
        HA = None if after is None else HEADS[after]
        looped = before is not None and LOOPED[before]
        normed = before in (1, 2)
        linear = after == 2
        with ExitStack() as ph, nc.Block() as block:
            xT = [sbuf(ph, f"{tag}xT{k}", [P, 2, P], F32) for k in range(DEPTH["xT"])] if after is not None else None
            node = [sbuf(ph, f"{tag}node{k}", [P, D], F32) for k in range(DEPTH["node"])]
            if before is not None:
                value = [sbuf(ph, f"{tag}value{k}", [P, D], F32) for k in range(DEPTH["value"])]
                share = sbuf(ph, tag + "share", [P, BLOCKS * HB], F32)
                sh3 = share[:].rearrange("p (b h) -> p b h", h=HB)
                calc = [sbuf(ph, f"{tag}calc{k}", [P, BLOCKS * HB], F32) for k in range(4)]
                c3 = [c[:].rearrange("p (b h) -> p b h", h=HB) for c in calc]
            if before is None:
                tables_start, tables_on_pool, tables_on_dve, tables_first_blocks, tables_columns = step_tables(ph)
            if looped:
                looprow = [sbuf(ph, f"{tag}looprow{k}", [P, D], F32) for k in range(DEPTH["looprow"])]
                loopterm = [sbuf(ph, f"{tag}loopterm{k}", [P, D], F32) for k in range(DEPTH["loopterm"])]
                own = sbuf(ph, tag + "own", [P, BLOCKS * HB], F32)
                own3 = own[:].rearrange("p (b h) -> p b h", h=HB)
            if normed:
                resrow = [sbuf(ph, f"{tag}resrow{k}", [P, D], F32) for k in range(DEPTH["resrow"])]
                bias_bc = sbuf(ph, tag + "bias_bc", [P, D], F32)
                stats = [sbuf(ph, f"{tag}stats{k}", [P, 6], F32) for k in range(DEPTH["value"])]
                mv = [sbuf(ph, f"{tag}mv{k}", [P, 2], F32) for k in range(DEPTH["value"])]
                rstd = [sbuf(ph, f"{tag}rstd{k}", [P, 3], F32) for k in range(DEPTH["value"])]
            if before == 0:
                bias_col = sbuf(ph, tag + "bias_col", [P, 2], F32)
            if after is not None:
                WA = D + 2 * HA
                wmat = sbuf(ph, tag + "wmat", [P, 2, WA], F32)
                attb = sbuf(ph, tag + "attb", [P, 2, D], F32)
                prod = sbuf(ph, tag + "prod", [P, 2, D], F32)
                row = [sbuf(ph, f"{tag}row{k}", [P, WA], F32) for k in range(DEPTH["row"])]
                pt = [psum(ph, f"{tag}pt{k}", [P, 512]) for k in range(2)]
                pm = [psum(ph, f"{tag}pm{k}", [P, 512]) for k in range(3)]
            if linear:
                wlin = sbuf(ph, tag + "wlin", [P, 2, D], F32)
                wlinT = sbuf(ph, tag + "wlinT", [P, 2, D], F32)
                wall = sbuf(ph, tag + "wall", [P, 2, WA], F32)
                blin_col = sbuf(ph, tag + "blin_col", [P, 2], F32)
                bias_row = sbuf(ph, tag + "bias_row", [1, D + WA], F32)
                bias_hml = sbuf(ph, tag + "bias_hml", [1, 3, D + WA], BF16)
                bias_parts = sbuf(ph, tag + "bias_parts", [2 * 32 + 1, D + WA], BF16)
                sum_parts = sbuf(ph, tag + "sum_parts", [2 * 32 + 1, P], BF16)
                resid = [sbuf(ph, f"{tag}resid{k}", [P, D], F32) for k in range(DEPTH["resid"])]
                pr = [psum(ph, f"{tag}pr{k}", [P, 512]) for k in range(3)]
                pw = pr
            weights = wall if linear else wmat if after is not None else None

            ad32 = sbuf(ph, tag + "ad32", [P, BLOCKS * 8], F32)
            ad3 = ad32[:].rearrange("p (b h) -> p b h", h=8)

            def buf(kind, b):
                return kind[b % len(kind)]

            def free(engine, s_reader, b, kind):
                if b >= len(kind):
                    engine.wait_ge(s_reader, b - len(kind) + 1)

            def heads(ap, b, H):
                return ap.rearrange("p (h c) -> p h c", h=H)

            def over(f3, b, H):
                return f3[:, b, :].unsqueeze(2).to_broadcast([P, H, D // H])

            n_w = 0
            def load_constants(q):
                n = 0
                with nc.allow_non_contiguous_dma(reason="a bias in columns, once"):
                    if after is not None:
                        q.dma_start(wmat[:, :, 0:D], t[f"w{after}"].rearrange("(k p) n -> p k n", p=P)).then_inc(s["w"], 16)
                        q.dma_start(attb[:], t[f"att{after}"].rearrange("(o k) n -> o k n", o=1).to_broadcast([P, 2, D])
                                    ).then_inc(s["w"], 16)
                        n += 2
                    if linear:
                        q.dma_start(wlin[:], t["w_lin"].rearrange("(k p) n -> p k n", p=P)).then_inc(s["w"], 16)
                        q.dma_start(blin_col[:], t["b_lin"].rearrange("o (k p) -> p (o k)", p=P)).then_inc(s["w"], 16)
                        q.dma_start(bias_row[:, 0:D], t["b_lin"]).then_inc(s["w"], 16)
                        n += 3
                    if before == 0:
                        q.dma_start(bias_col[:], t["bias0"].rearrange("o (k p) -> p (o k)", p=P)).then_inc(s["w"], 16)
                        n += 1
                    if normed:
                        q.dma_start(bias_bc[:], t[f"bias{before}"].to_broadcast([P, D])).then_inc(s["w"], 16)
                        n += 1
                return 16 * n
            N_CONST = 16 * ((2 if after is not None else 0) + (3 if linear else 0) + (1 if before in (0, 1, 2) else 0))

            def rows_of(b):
                return slice(b * P, (b + 1) * P)

            def load(q, b):
                if before is None:
                    free(q, s["turned"], b, node)
                    q.dma_start(buf(node, b)[:], t["x_pad"][rows_of(b), :]).then_inc(buf(s_node, b), 16)
                if looped:
                    free(q, s["loop_term"], b, looprow)
                    q.dma_start(buf(looprow, b)[:], table[before][rows_of(b), 0:D]).then_inc(buf(s_loop, b), 16)
                if normed:
                    free(q, s["loop_term"] if looped else s["value"], b, resrow)
                    src = t["x_pad"] if before == 1 else resid_dram
                    q.dma_start(buf(resrow, b)[:], src[rows_of(b), :]).then_inc(buf(s_res, b), 16)

            def moved(engine, sems, b):
                engine.wait_ge(buf(sems, b), 16 * (b // len(sems) + 1))

            def all_moved(engine, sems):
                for b in range(BLOCKS - len(sems), BLOCKS):
                    moved(engine, sems, b)

            @block.sync
            def _(sp):
                if before is None:
                    tables_start(sp)
                load_constants(sp)
                for b in range(BLOCKS):
                    load(sp, b)

            @block.scalar
            def _(act):
                if before is not None and looped:
                    act.wait_ge(s["prep"], 1)
                    nc.scalar.activation(share[:], calc[0][:], ACT.Exp)
                    nc.scalar.activation(own[:], calc[1][:], ACT.Exp).then_inc(s["prep_act"], 1)

                def root(b):
                    act.wait_ge(s["mean"], b + 1)
                    free(act, s["rinv"], b, rstd)
                    nc.scalar.activation(buf(rstd, b)[:, 0:1], buf(mv, b)[:, 1:2], ACT.Sqrt, bias=eps_col[:, 0:1]
                                         ).then_inc(s["root"], 1)

                def x_turned(b):
                    act.wait_ge(s["turned"], b + 1)
                    free(act, s["mm"], b, xT)
                    if before == 0:
                        if b == 0:
                            act.wait_ge(s["w"], N_CONST)
                        for k in range(2):
                            last = nc.scalar.activation(buf(xT, b)[:, k, :], pt[b % 2][:, k * P:(k + 1) * P], ACT.Relu,
                                                        bias=bias_col[:, k:k + 1])
                    else:
                        last = nc.scalar.copy(buf(xT, b)[:].rearrange("p k e -> p (k e)"), pt[b % 2][:, 0:D])
                    last.then_inc(s["xT"], 1)

                def table_row(b):
                    act.wait_ge(s["mm"], b + 1)
                    if b >= len(row):
                        moved(act, s_row, b - len(row))
                    free(act, s["att"], b, row)
                    nc.scalar.copy(buf(row, b)[:], buf(pm, b)[:, 0:WA]).then_inc(s["row"], 1)

                def take_attention(b):
                    act.wait_ge(s["row"], b + 1)
                    nc.scalar.copy(as3[:, b, 0:HA], buf(row, b)[:, D:D + HA])
                    nc.scalar.copy(ad3[:, b, 0:HA], buf(row, b)[:, D + HA:D + 2 * HA]).then_inc(s["att"], 1)

                def store_row(b):
                    act.wait_ge(s["row"], b + 1)
                    act.dma_start(table[after][rows_of(b), :], buf(row, b)[:, 0:D + HA]).then_inc(buf(s_row, b), 16)

                def store_resid(b):
                    act.wait_ge(s["resid"], b + 1)
                    act.dma_start(resid_dram[rows_of(b), :], buf(resid, b)[:]).then_inc(buf(s_rst, b), 16)

                def scale(b):
                    act.wait_ge(s["shift"], b + 1)
                    if b >= len(node):
                        moved(act, s_out, b - len(node))
                    nc.scalar.activation(buf(node, b)[:], buf(value, b)[:], ACT.Identity, bias=buf(rstd, b)[:, 2:3],
                                         scale=buf(rstd, b)[:, 1:2]).then_inc(s["node"], 1)

                def store_out(b):
                    act.wait_ge(s["node"], b + 1)
                    n = min(P, N_NODES - b * P)
                    act.dma_start(t["out"][b * P:b * P + n, :], buf(node, b)[0:n, :]).then_inc(buf(s_out, b), 16)

                steps = []
                if normed:
                    steps.append((0, root))
                if after is not None:
                    lag = 6 if normed else 0
                    steps += [(lag, x_turned), (lag + 2 if normed else lag + 1, table_row), (lag + 3, store_row)]
                else:
                    steps += [(4, scale), (6, store_out)]
                if before is None:
                    steps.append((lag + 2, take_attention))
                if linear:
                    steps.append((10, store_resid))
                for i in range(BLOCKS + 10):
                    for lag, step in steps:
                        if 0 <= i - lag < BLOCKS:
                            step(i - lag)
                all_moved(act, s_row if after is not None else s_out)
                if linear:
                    all_moved(act, s_rst)

            @block.gpsimd
            def _(pool):
                if before is None:
                    tables_on_pool(pool)
                if looped:
                    pool.wait_ge(s["prep"], 2)
                    if normed:
                        pool.wait_ge(s["w"], N_CONST)
                    for b in range(BLOCKS):
                        term = buf(loopterm, b)[:]
                        moved(pool, s_loop, b)
                        free(pool, s["value"], b, loopterm)
                        ins = nc.gpsimd.tensor_tensor(heads(term, b, HB), heads(buf(looprow, b)[:], b, HB),
                                                      over(own3, b, HB), ALU.mult)
                        if normed:
                            for n, other in enumerate((bias_bc, buf(resrow, b))):
                                ins.then_inc(s["chain_p"], 1)
                                if n:
                                    moved(pool, s_res, b)
                                pool.wait_ge(s["chain_p"], 2 * b + n + 1)
                                ins = nc.gpsimd.tensor_tensor(term, term, other[:], ALU.add)
                        ins.then_inc(s["loop_term"], 1)
                elif normed:
                    pool.wait_ge(s["w"], N_CONST)
                    for i in range(BLOCKS + 3):
                        if i < BLOCKS:
                            v = buf(value, i)[:]
                            pool.wait_ge(s["v1"], i + 1)
                            nc.gpsimd.tensor_tensor(v, v, bias_bc[:], ALU.add).then_inc(s["v2"], 1)
                        if i >= 3:
                            v = buf(value, i - 3)[:]
                            pool.wait_ge(s["v3"], i - 2)
                            moved(pool, s_res, i - 3)
                            nc.gpsimd.tensor_tensor(v, v, buf(resrow, i - 3)[:], ALU.add).then_inc(s["value"], 1)

            @block.vector
            def _(dve):
                link = link_on(dve, s["chain"])
                if before is not None:
                    den, top_a = acc3[:, :, D:D + HB], acc3[:, :, D + HB:D + 2 * HB]
                if looped:
                    a_src, a_dst = as3[:, :, 0:HB], ad3[:, :, 0:HB]
                    link(nc.vector.tensor_tensor(a_dst, parts4[:, :, 0:HB, 2], parts4[:, :, 0:HB, 1], ALU.add))
                    link(nc.vector.tensor_tensor(a_dst, a_dst, parts4[:, :, 0:HB, 0], ALU.add))
                    link(nc.vector.tensor_scalar(c3[0], den, 0.0, -BIG, ALU.is_equal, ALU.mult))
                    link(nc.vector.tensor_tensor(c3[0], c3[0], top_a, ALU.add))
                    link(nc.vector.tensor_tensor(c3[1], c3[0], a_src, ALU.max))
                    link(nc.vector.tensor_tensor(c3[2], c3[0], a_dst, ALU.add))
                    link(nc.vector.tensor_tensor(c3[3], a_src, a_dst, ALU.add))
                    link(nc.vector.tensor_tensor(c3[1], c3[1], a_dst, ALU.add))
                    for c in (1, 2, 3):
                        link(nc.vector.scalar_tensor_tensor(c3[c], c3[c], SLOPE, c3[c], ALU.mult, ALU.max))
                    link(nc.vector.tensor_tensor(c3[0], c3[2], c3[1], ALU.subtract))
                    link(nc.vector.tensor_tensor(c3[1], c3[3], c3[1], ALU.subtract))
                    link(nc.vector.tensor_scalar(c3[0], c3[0], 0.0, None, ALU.min))
                    nc.vector.tensor_scalar(c3[1], c3[1], 0.0, None, ALU.min).then_inc(s["prep"], 1)
                    dve.wait_ge(s["prep_act"], 1)
                    link(nc.vector.tensor_tensor(c3[2], den, sh3, ALU.mult))
                    link(nc.vector.tensor_tensor(c3[2], c3[2], own3, ALU.add))
                    link(nc.vector.tensor_scalar(c3[2], c3[2], 1e-16, None, ALU.max))
                    link(nc.vector.reciprocal(c3[3], c3[2]))
                    link(nc.vector.tensor_tensor(sh3, sh3, c3[3], ALU.mult))
                    nc.vector.tensor_tensor(own3, own3, c3[3], ALU.mult).then_inc(s["prep"], 1)
                    dve.wait_ge(s["prep"], 2)
                elif before is not None:
                    link(nc.vector.scalar_tensor_tensor(c3[0], den, 0.0, den, ALU.is_equal, ALU.add))
                    link(nc.vector.reciprocal(sh3, c3[0]))
                if after is not None:
                    dve.wait_ge(s["w"], N_CONST)
                    C = D // HA
                    for k in range(2):
                        link(nc.vector.tensor_tensor(prod[:], wmat[:, :, 0:D],
                                                     attb[:, k, :].unsqueeze(1).to_broadcast([P, 2, D]), ALU.mult))
                        link(nc.vector.tensor_reduce(wmat[:, :, D + k * HA:D + (k + 1) * HA],
                                                     prod[:].rearrange("p k (h c) -> p k h c", c=C), AX.X, ALU.add))
                if linear:
                    dve.sem_inc(s["prep_pe"], 1)
                    for k in range(2):
                        dve.wait_ge(s["fold"], 1 + k)
                        last = nc.vector.tensor_copy(wlinT[:, k, :], pw[k][:, 0:D])
                    last.then_inc(s["prep_pe"], 1)
                    dve.wait_ge(s["fold"], 3)
                    for k in range(2):
                        last = nc.vector.tensor_copy(wall[:, k, :], pw[k][:, 0:WA])
                    last.then_inc(s["prep_pe"], 1)
                    dve.wait_ge(s["fold"], 4)
                    link(nc.vector.tensor_copy(bias_row[:, D:], pw[0][0:1, 0:WA]))
                    nc.vector.memset(bias_parts[:], 0.0)
                    link(nc.vector.memset(sum_parts[:], 0.0))
                    for k in range(3):
                        link(nc.vector.tensor_copy(bias_hml[:, k, :], bias_row[:]))
                        if k < 2:
                            link(nc.vector.tensor_tensor(bias_row[:], bias_row[:], bias_hml[:, k, :], ALU.subtract))
                        nc.vector.memset(sum_parts[32 * k:32 * k + 1, :], 1.0)
                        last = nc.vector.tensor_copy(bias_parts[32 * k:32 * k + 1, :], bias_hml[:, k, :])
                    last.then_inc(s["prep_pe"], 1)
                elif after is not None:
                    dve.sem_inc(s["prep_pe"], 1)
                if normed:
                    dve.wait_ge(s["w"], N_CONST)

                def value_share(b):
                    free(dve, s["node"] if normed else s["turned"], b, value)
                    num = acc[:, b * ACC_W:b * ACC_W + D]
                    nc.vector.tensor_tensor(heads(buf(value, b)[:], b, HB), heads(num, b, HB), over(sh3, b, HB), ALU.mult
                                            ).then_inc(s["v1"], 1)

                def value_add(b):
                    v = buf(value, b)[:]
                    dve.wait_ge(s["v1"], b + 1)
                    if looped:
                        dve.wait_ge(s["loop_term"], b + 1)
                        nc.vector.tensor_tensor(v, v, buf(loopterm, b)[:], ALU.add).then_inc(s["value"], 1)

                def value_leaky(b):
                    v = buf(value, b)[:]
                    dve.wait_ge(s["v2"], b + 1)
                    nc.vector.scalar_tensor_tensor(v, v, OUT_SLOPE, v, ALU.mult, ALU.max).then_inc(s["v3"], 1)

                def statistics(b):
                    dve.wait_ge(s["value"], b + 1)
                    nc.vector.bn_stats(buf(stats, b)[:], buf(value, b)[:]).then_inc(s["stats"], 1)

                def mean(b):
                    dve.wait_ge(s["stats"], b + 1)
                    nc.vector.bn_aggr(buf(mv, b)[:], buf(stats, b)[:]).then_inc(s["mean"], 1)

                def rinv(b):
                    dve.wait_ge(s["root"], b + 1)
                    nc.vector.reciprocal(buf(rstd, b)[:, 1:2], buf(rstd, b)[:, 0:1]).then_inc(s["rinv"], 1)

                def shift(b):
                    dve.wait_ge(s["rinv"], b + 1)
                    nc.vector.scalar_tensor_tensor(buf(rstd, b)[:, 2:3], buf(mv, b)[:, 0:1], -1.0, buf(rstd, b)[:, 1:2],
                                                   ALU.mult, ALU.mult).then_inc(s["shift"], 1)

                def normalise(b):
                    dve.wait_ge(s["rinv"], b + 1)
                    free(dve, s["turned"], b, node)
                    free(dve, s["resid"], b, node)
                    nc.vector.tensor_scalar(buf(node, b)[:], buf(value, b)[:], buf(mv, b)[:, 0:1], buf(rstd, b)[:, 1:2], ALU.subtract, ALU.mult
                                            ).then_inc(s["node"], 1)

                def attention(b):
                    dve.wait_ge(s["row"], b + 1)
                    nc.vector.tensor_copy(as3[:, b, 0:HA], buf(row, b)[:, D:D + HA])
                    nc.vector.tensor_copy(ad3[:, b, 0:HA], buf(row, b)[:, D + HA:D + 2 * HA]).then_inc(s["att"], 1)

                def residual(b):
                    dve.wait_ge(s["mm"], b + 1)
                    if b >= len(resid):
                        moved(dve, s_rst, b - len(resid))
                    nc.vector.tensor_tensor(buf(resid, b)[:], buf(node, b)[:], buf(pr, b)[:, 0:D], ALU.add).then_inc(s["resid"], 1)

                chain = []
                if before is not None:
                    chain.append(value_share)
                if looped:
                    chain.append(value_add)
                elif before is not None:
                    chain += [None, None, value_leaky, None, None]
                if normed:
                    chain += [statistics, mean, None, None, rinv, normalise if after is not None else shift]
                steps = [(lag, step) for lag, step in enumerate(chain) if step]
                if before is None:
                    tables_on_dve(dve)
                elif after is not None:
                    steps.append((len(chain) + 4, attention))
                if linear:
                    steps.append((len(chain) + 3, residual))
                for i in range(BLOCKS + len(chain) + 4):
                    for lag, step in reversed(steps):
                        if 0 <= i - lag < BLOCKS:
                            step(i - lag)
                if after is not None:
                    dve.wait_ge(s["att"], BLOCKS)
                    rest = ad3[:, :, 0:HA]
                    for k in range(3):
                        link(nc.vector.tensor_copy(parts4[:, :, 0:HA, k], rest))
                        if k < 2:
                            link(nc.vector.tensor_tensor(rest, rest, parts4[:, :, 0:HA, k], ALU.subtract))

            @block.tensor
            def _(pe):
                if after is None:
                    return
                x_now = node if (before is None or normed) else value
                x_ready = (s["node"] if normed else s["value"]) if before is not None else None
                if before is None:
                    pe.wait_ge(s_const, 2)
                pe.wait_ge(s["prep_pe"], 1)
                if linear:
                    for jc in range(2):
                        for kc in range(2):
                            last = nc.tensor.transpose(pw[jc][:, kc * P:(kc + 1) * P], wlin[:, kc, jc * P:(jc + 1) * P],
                                                       ident[:])
                        last.then_inc(s["fold"], 1)
                    pe.wait_ge(s["prep_pe"], 2)
                    for kc in range(2):
                        for jc in range(2):
                            last = nc.tensor.matmul(pw[kc][:, 0:WA], wlinT[:, jc, kc * P:(kc + 1) * P], wmat[:, jc, :],
                                                    start=(jc == 0), stop=(jc == 1))
                    last.then_inc(s["fold"], 1)
                    pe.wait_ge(s["prep_pe"], 3)
                    for jc in range(2):
                        last = nc.tensor.matmul(pw[0][0:1, 0:WA], blin_col[:, jc:jc + 1], wmat[:, jc, :],
                                                start=(jc == 0), stop=(jc == 1))
                    last.then_inc(s["fold"], 1)
                    pe.wait_ge(s["prep_pe"], 4)

                def turn_block(b):
                    if before is None:
                        moved(pe, s_node, b)
                    else:
                        pe.wait_ge(x_ready, b + 1)
                    if b >= 2:
                        pe.wait_ge(s["xT"], b - 1)
                    for k in range(2):
                        last = nc.tensor.transpose(pt[b % 2][:, k * P:(k + 1) * P], buf(x_now, b)[:, k * P:(k + 1) * P],
                                                   ident[:])
                    last.then_inc(s["turned"], 1)

                def multiply(b):
                    pe.wait_ge(s["xT"], b + 1)
                    free(pe, s["row"], b, pm)
                    if linear:
                        free(pe, s["resid"], b, pr)
                    if linear:
                        for k in range(2):
                            nc.tensor.matmul(buf(pr, b)[:, 0:D], buf(xT, b)[:, k, :], wlin[:, k, :], start=(k == 0), stop=False)
                        nc.tensor.matmul(buf(pr, b)[:, 0:D], sum_parts[:], bias_parts[:, 0:D], start=False, stop=True)
                    for k in range(2):
                        last = nc.tensor.matmul(buf(pm, b)[:, 0:WA], buf(xT, b)[:, k, :], weights[:, k, :],
                                                start=(k == 0), stop=(k == 1 and not linear))
                    if linear:
                        last = nc.tensor.matmul(buf(pm, b)[:, 0:WA], sum_parts[:], bias_parts[:, D:], start=False, stop=True)
                    last.then_inc(s["mm"], 1)

                for i in range(BLOCKS + 1):
                    if i < BLOCKS:
                        turn_block(i)
                    if i >= 1:
                        multiply(i - 1)
                    if before is None and i == TABLES_FIRST:
                        tables_first_blocks(pe)
                    if before is None and i == TABLES_COLUMNS:
                        tables_columns(pe)

    STAGES = ("compact", "srcT", "onehotT", "onehot", "masked", "scan", "seg", "rowsum", "rowin", "carry", "colsum",
              "tail_sum", "tail", "top1", "top", "topT", "topread", "lookup", "adst", "y1", "l1", "y2", "l2", "dist",
              "gap", "expo", "first_y", "first_l", "first_d", "fdist", "fmat", "factor", "rescaled",
              "msg0", "msg1", "msg2", "msg3", "settled")
    st = {n: sem("e_" + n) for n in STAGES}
    s_mm = [sem(f"e_mm{q}") for q in range(4)]
    s_late, s_late_add = sem("e_late"), sem("e_late_add")
    s_clear = sem("e_clear")
    s_start = sem("e_start")
    s_apart = sem("e_apart")

    def edge_phase(L):
        H = HEADS[L]
        C = D // H
        HG = H * G
        TW = D + H
        MW = D + 2 * H
        W0 = L * WINDOWS
        N_LOAD = 16 * (5 + H)
        s_idx, s_gat, s_ld = ([sem(f"e{L}_{n}{k}") for k in range(BUFS)] for n in ("idx", "gathered", "loaded"))
        tag = f"e{L}_"
        with ExitStack() as ph, nc.Block() as block:
            rows = [sbuf(ph, f"{tag}rows{k}", [P, G, MW], F32) for k in range(BUFS)]
            idx = [sbuf(ph, f"{tag}idx{k}", [P, G], I32) for k in range(BUFS)]
            col = [sbuf(ph, f"{tag}col{k}", [P, 2, G], BF16) for k in range(BUFS)]
            onehot = sbuf(ph, tag + "onehot", [P, G, P], F32)
            onehotT = [sbuf(ph, f"{tag}onehotT{k}", [P, G * P], BF16) for k in range(BUFS)]
            mask = [sbuf(ph, f"{tag}mask{k}", [P, MASKS, P], BF16) for k in range(BUFS)]
            passf = [sbuf(ph, f"{tag}passf{k}", [1, H, G], F32) for k in range(BUFS)]
            passb = [sbuf(ph, f"{tag}passb{k}", [1, H, G], F32) for k in range(BUFS)]
            passn = [sbuf(ph, f"{tag}passn{k}", [1, H, 1], F32) for k in range(BUFS)]
            inf, inb, outf, outb = (sbuf(ph, tag + n, [1, H, G], F32) for n in ("inf", "inb", "outf", "outb"))
            nxt = sbuf(ph, tag + "nxt", [1, H, 1], F32)
            tail = sbuf(ph, tag + "tail", [1, H, 1], F32)
            srcc = sbuf(ph, tag + "srcc", [P, H, G], F32)
            srcm, fwd, bwd, seg, top = (sbuf(ph, tag + n, [HG, P], F32) for n in ("srcm", "fwd", "bwd", "seg", "top"))
            adst, l1, l2, gap = (sbuf(ph, tag + n, [P, G, H], F32) for n in ("adst", "l1", "l2", "gap"))
            fy, fl, fd, fdiff = (sbuf(ph, tag + n, [1, H], F32) for n in ("fy", "fl", "fd", "fdiff"))
            fcont = sbuf(ph, tag + "fcont", [1, 1], F32)
            factor = sbuf(ph, tag + "factor", [P, H], F32)
            p_mm = psum(ph, tag + "p_mm", [P, REGIONS * BANK])
            p_src = psum(ph, tag + "p_src", [P, 512])
            p_look = psum(ph, tag + "p_look", [P, 512])
            p_top = psum(ph, tag + "p_top", [P, 512])
            p_small = psum(ph, tag + "p_small", [P, 512])
            flat = lambda a: a[:].rearrange("o h g -> o (h g)")

            def walk(engine, body):
                def at(w, k, turns, first=False):
                    regs = {}
                    def ago(n):
                        if n not in regs:
                            count = w + (W0 + 1 - n)
                            regs[n] = count if isinstance(w, int) else engine.snap(count)
                        return regs[n]
                    if isinstance(w, int):
                        body(w, k, turns, ago, first)
                    else:
                        body(w if engine is nc.gpsimd else engine.snap(w), k, engine.snap(turns), ago, first)
                for w in range(BUFS):
                    at(w, w, 1, first=w == 0)
                with engine.Fori(1, WINDOWS // BUFS) as i:
                    for k in range(BUFS):
                        at(i * BUFS + k, k, i + 1)
                for w in range(WINDOWS // BUFS * BUFS, WINDOWS):
                    at(w, w % BUFS, w // BUFS + 1)

            def wait(engine, s, n):
                if not (isinstance(n, int) and n <= 0):
                    engine.wait_ge(s, n)

            def wait_apart(engine, s, n):
                if not (isinstance(n, int) and n <= 0):
                    engine.wait_ge(s, n)
                    engine.sem_inc(s_apart, 1)

            def count(engine, n):
                return n if isinstance(n, int) else engine.snap(n)

            def words(engine, row, start, n):
                return nc.values_load_multi_w_load_instructions(
                    off_row[row:row + 1, bass.ds(start, n)], engines=[engine.engine], min_val=0,
                    max_val=((REGIONS - 1) * BANK, (BLOCKS - 1) * ADS_W, (BLOCKS - 1) * ACC_W, (BLOCKS - 1) * ACC_W)[row],
                    skip_runtime_bounds_check_because="phase 0 clamps the block")[1]

            @block.gpsimd
            def _(pool):
                def body(w, k, turns, ago, first):
                    pool.wait_ge(s_idx[k], turns * 16)
                    wait(pool, st["settled"], ago(BUFS - 1))
                    pool.sem_inc(s_apart, 1)
                    for g in range(G):
                        pool.indirect_dma_start(rows[k][:, g, 0:TW], None, table[L],
                                                bass.IndirectOffsetOnAxis(ap=idx[k][:, g:g + 1], axis=0)
                                                ).then_inc(s_gat[k], 16)
                walk(pool, body)

            @block.sync
            def _(sp):
                sp.wait_ge(s_start, L + 1)

                def body(w, k, turns, ago, first):
                    wait_apart(sp, st["compact"], ago(BUFS))
                    sp.dma_start(idx[k][:], src_dram[bass.ds(w, 1), :, :].rearrange("w p g -> p (w g)")
                                 ).then_inc(s_idx[k], 16)
                    wait_apart(sp, st["settled"], ago(BUFS - 1))
                    sp.dma_start(col[k][:].rearrange("p c g -> p (c g)"),
                                 col_dram[bass.ds(w, 1), :, :, :].rearrange("w p c g -> p (w c g)")).then_inc(s_ld[k], 16)
                    sp.dma_start(onehotT[k][:], rel_dram[bass.ds(w * G, G), :].rearrange("(o g) e -> o (g e)", o=1)
                                 .to_broadcast([P, G * P])).then_inc(s_ld[k], 16)
                    for h in range(H):
                        sp.dma_start(mask[k][h * G:(h + 1) * G, :, :].rearrange("g m e -> g (m e)"),
                                     mask_dram[bass.ds(w * G, G), :]).then_inc(s_ld[k], 16)
                    for d, tile, o, n, at in ((0, passf, 1, G - 1, 0), (0, passn, 0, 1, G - 1), (1, passb, 0, G - 1, 1)):
                        sp.dma_start(tile[k][0:1, :, o:o + n], pass_dram[d:d + 1, bass.ds(w * G + at, n)].unsqueeze(1)
                                     .to_broadcast([1, H, n])).then_inc(s_ld[k], 16)
                walk(sp, body)

            @block.scalar
            def _(act):
                def body(w, k, turns, ago, first):
                    now, past = ago(0), ago(1)
                    act.wait_ge(s_gat[k], turns * (16 * G))
                    wait(act, st["srcT"], past)
                    nc.scalar.copy(srcc[:], rows[k][:, :, D:D + H].rearrange("p g h -> p h g")).then_inc(st["compact"], 1)
                    act.wait_ge(st["gap"], now)
                    nc.scalar.activation(rows[k][:, :, D:D + H], gap[:], ACT.Exp).then_inc(st["expo"], 1)
                    act.wait_ge(st["fmat"], now)
                    wait(act, st["rescaled"], past)
                    nc.scalar.activation(factor[:], p_small[:, 264:264 + H], ACT.Exp).then_inc(st["factor"], 1)
                walk(act, body)

            @block.tensor
            def _(pe):
                def product(g, k, region, done):
                    if g == 0:
                        wait_apart(pe, st["msg0"], done)
                        for r in range(REGIONS):
                            nc.tensor.matmul(p_mm[:, r * BANK:r * BANK + MW], zeros[:, 0:P], zeros[:, 0:MW], start=True,
                                             stop=False, skip_group_check=True)
                    elif g % 4 == 0:
                        pe.wait_ge(st[f"msg{g // 4}"], done)
                    ins = nc.tensor.matmul(p_mm[:, bass.ds(region, MW)], onehot[:, g, :], rows[k][:, g, :], start=False,
                                           stop=True, skip_group_check=True)
                    if g % 4 == 3:
                        ins.then_inc(s_mm[g // 4], 1)

                def late_products(k, slow, done):
                    with pe.If(slow != 0):
                        for g in range(G):
                            wait_apart(pe, s_late_add, count(pe, (done - 1) * G + (g + 1)))
                            nc.tensor.matmul(p_mm[:, 0:MW], onehot[:, g, :], rows[k][:, g, :], start=True, stop=True
                                             ).then_inc(s_late, 1)
                    with pe.Else():
                        pe.sem_inc(s_late, G)

                def body(w, k, turns, ago, first):
                    now, past = ago(0), ago(1)
                    if not first:
                        regions = words(pe, 0, (w - 1) * G, G)
                        slow, = words(pe, 3, (w - 1) * WIN + REGIONS, 1)
                    def products(a, b):
                        if not first:
                            for g in range(a, b):
                                product(g, (k - 1) % BUFS, regions[g], past)
                    products(0, 4)
                    wait_apart(pe, st["compact"], now)
                    wait_apart(pe, st["masked"], past)
                    nc.tensor.transpose(p_src[0:HG, 0:P], srcc[:].rearrange("p h g -> p (h g)"), ident[:]
                                        ).then_inc(st["srcT"], 1)
                    products(4, 6)
                    wait_apart(pe, st["scan"], now)
                    wait_apart(pe, st["factor"], past)
                    for dst, col, o in ((0, fwd[:, P - 1:P], 0), (1, bwd[:, 0:1], P)):
                        last = nc.tensor.matmul(p_small[0:1, o:o + HG], col, ident[0:HG, 0:HG], start=True, stop=True)
                    last.then_inc(st["rowsum"], 1)
                    offs = words(pe, 1, w * G, G)
                    pe.wait_ge(st["onehotT"], now)
                    wait(pe, st["adst"], past)
                    for g in range(G):
                        last = nc.tensor.matmul(p_look[:, g * 3 * H:(g + 1) * 3 * H], onehotT[k][:, g * P:(g + 1) * P],
                                                ad_parts[:, bass.ds(offs[g], 3 * H)], start=True, stop=True)
                    last.then_inc(st["lookup"], 1)
                    products(6, 9)
                    wait_apart(pe, st["carry"], now)
                    for o, src in ((256, outf), (257, outb)):
                        last = nc.tensor.matmul(p_small[0:HG, o:o + 1], flat(src), ones_row[0:1, 0:1],
                                                start=True, stop=True)
                    last.then_inc(st["colsum"], 1)
                    products(9, 12)
                    wait_apart(pe, st["top"], now)
                    wait_apart(pe, st["topread"], past)
                    nc.tensor.transpose(p_top[:, 0:HG], top[:], ident[0:HG, 0:HG]).then_inc(st["topT"], 1)
                    products(12, 16)
                    if not first:
                        late_products((k - 1) % BUFS, slow, past)
                    wait_apart(pe, st["fdist"], now)
                    nc.tensor.matmul(p_small[:, 264:264 + H], onehot[0:1, 0, :], fdiff[:], start=True, stop=True
                                     ).then_inc(st["fmat"], 1)
                walk(pe, body)
                regions = words(pe, 0, (WINDOWS - 1) * G, G)
                slow, = words(pe, 3, (WINDOWS - 1) * WIN + REGIONS, 1)
                for g in range(G):
                    product(g, (WINDOWS - 1) % BUFS, regions[g], W0 + WINDOWS)
                late_products((WINDOWS - 1) % BUFS, slow, W0 + WINDOWS)

            @block.vector
            def _(dve):
                def add(r, off, done):
                    if r == 0:
                        dve.wait_ge(s_mm[3], done)
                        dve.wait_ge(st["rescaled"], done)
                    sums = acc[:, bass.ds(off, MW)]
                    nc.vector.tensor_tensor(sums, sums, p_mm[:, r * BANK:r * BANK + MW], ALU.add)

                def one_hot(k, nodes, q):
                    return nc.vector.tensor_tensor(
                        onehot[:, 4 * q:4 * q + 4, :], col[k][:, 0, 4 * q:4 * q + 4].unsqueeze(2).to_broadcast([P, 4, P]),
                        nodes[:].unsqueeze(1).to_broadcast([P, 4, P]), ALU.is_equal)

                def late_adds(w, k, slow, done, again=True):
                    with dve.If(slow != 0):
                        for q in range(4):
                            ins = one_hot(k, beyond_d, q)
                        ins.then_inc(s_late_add, 1)
                        for g in range(G):
                            off, = words(dve, 2, w * G + g, 1)
                            wait_apart(dve, s_late, count(dve, (done - 1) * G + (g + 1)))
                            sums = acc[:, bass.ds(off, MW)]
                            ins = nc.vector.tensor_tensor(sums, sums, p_mm[:, 0:MW], ALU.add)
                            if g < G - 1:
                                ins.then_inc(s_late_add, 1)
                        if again:
                            for q in range(3):
                                one_hot((k + 1) % BUFS, iota_d, q)
                    with dve.Else():
                        dve.sem_inc(s_late_add, G)

                def body(w, k, turns, ago, first):
                    now, past = ago(0), ago(1)
                    if first:
                        off = words(dve, 3, 0, 1)[0]
                    else:
                        words_read = words(dve, 3, (w - 1) * WIN, WIN + 1)
                        offs, slow, off = words_read[:REGIONS], words_read[REGIONS], words_read[WIN]
                    m = mask[k]

                    def one_hots(q):
                        if not first:
                            dve.wait_ge(s_mm[q], past)
                        return one_hot(k, iota_d, q)

                    dve.wait_ge(s_ld[k], turns * N_LOAD)
                    dve.wait_ge(st["srcT"], now)
                    nc.vector.tensor_tensor(srcm[:], p_src[0:HG, 0:P], m[0:HG, 0, :], ALU.add).then_inc(st["masked"], 1)
                    dve.wait_ge(st["masked"], now)
                    nc.vector.tensor_tensor_scan(fwd[:], m[0:HG, 1, :], srcm[:], -BIG, ALU.add, ALU.max)
                    nc.vector.tensor_tensor_scan(bwd[:, ::-1], m[0:HG, 2, ::-1], srcm[:, ::-1], -BIG, ALU.add, ALU.max
                                                 ).then_inc(st["scan"], 1)
                    nc.vector.tensor_scalar(onehotT[k][:], onehotT[k][:], pidx[:, 0:1], None, ALU.is_equal
                                            ).then_inc(st["onehotT"], 1)
                    dve.wait_ge(st["scan"], now)
                    nc.vector.tensor_tensor(seg[:], fwd[:], bwd[:], ALU.max).then_inc(st["seg"], 1)
                    dve.wait_ge(st["rowsum"], now)
                    rf = p_small[0:1, 0:HG].rearrange("o (h g) -> o h g", g=G)
                    rb = p_small[0:1, P:P + HG].rearrange("o (h g) -> o h g", g=G)
                    if first:
                        nc.vector.memset(inf[:, :, 0:1], -BIG)
                    else:
                        nc.vector.tensor_copy(inf[:, :, 0:1], nxt[:])
                    nc.vector.tensor_copy(inf[:, :, 1:G], rf[:, :, 0:G - 1])
                    nc.vector.tensor_copy(tail[:], rf[:, :, G - 1:G])
                    nc.vector.tensor_copy(inb[:, :, 0:G - 1], rb[:, :, 1:G]).then_inc(st["rowin"], 1)
                    one_hots(0)
                    dve.wait_ge(st["rowin"], now)
                    nc.vector.tensor_tensor_scan(flat(outf), flat(passf[k]), flat(inf), -BIG, ALU.add, ALU.max)
                    nc.vector.tensor_tensor_scan(flat(outb)[:, ::-1], flat(passb[k])[:, ::-1], flat(inb)[:, ::-1], -BIG,
                                                 ALU.add, ALU.max).then_inc(st["carry"], 1)
                    dve.wait_ge(st["carry"], now)
                    nc.vector.tensor_tensor(nxt[:], outf[:, :, G - 1:G], passn[k][:], ALU.add).then_inc(st["tail_sum"], 1)
                    dve.wait_ge(st["tail_sum"], now)
                    nc.vector.tensor_tensor(nxt[:], nxt[:], tail[:], ALU.max).then_inc(st["tail"], 1)
                    dve.wait_ge(st["lookup"], now)
                    nc.vector.tensor_reduce(adst[:].rearrange("p g h -> p (g h)"),
                                            p_look[:, 0:3 * HG].rearrange("p (n k) -> p n k", k=3), AX.X, ALU.add
                                            ).then_inc(st["adst"], 1)
                    dve.wait_ge(st["adst"], now)
                    nc.vector.tensor_tensor(l1[:], rows[k][:, :, D:D + H], adst[:], ALU.add).then_inc(st["y1"], 1)
                    dve.wait_ge(st["colsum"], now)
                    nc.vector.scalar_tensor_tensor(top[:], m[0:HG, 3, :], p_small[0:HG, 256:257], seg[:], ALU.add, ALU.max
                                                   ).then_inc(st["top1"], 1)
                    one_hots(1)
                    dve.wait_ge(st["top1"], now)
                    nc.vector.scalar_tensor_tensor(top[:], m[0:HG, 4, :], p_small[0:HG, 257:258], top[:], ALU.add, ALU.max
                                                   ).then_inc(st["top"], 1)
                    dve.wait_ge(st["y1"], now)
                    nc.vector.scalar_tensor_tensor(l1[:], l1[:], SLOPE, l1[:], ALU.mult, ALU.max).then_inc(st["l1"], 1)
                    dve.wait_ge(st["topT"], now)
                    top_e = p_top[:, 0:HG].rearrange("p (h g) -> p g h", g=G)
                    nc.vector.tensor_tensor(l2[:], top_e, adst[:], ALU.add).then_inc(st["y2"], 1)
                    nc.vector.tensor_tensor(rows[k][:, :, D + H:MW], top_e,
                                            col[k][:, 1, :].unsqueeze(2).to_broadcast([P, G, H]), ALU.mult
                                            ).then_inc(st["topread"], 1)
                    dve.wait_ge(st["y2"], now)
                    nc.vector.scalar_tensor_tensor(l2[:], l2[:], SLOPE, l2[:], ALU.mult, ALU.max).then_inc(st["l2"], 1)
                    one_hots(2)
                    dve.wait_ge(st["l2"], now)
                    wait(dve, st["expo"], past)
                    nc.vector.tensor_tensor(gap[:], l1[:], l2[:], ALU.subtract).then_inc(st["dist"], 1)
                    nc.vector.tensor_tensor(fy[:], inf[:, :, 0], adst[0:1, 0, :], ALU.add).then_inc(st["first_y"], 1)
                    nc.vector.tensor_tensor(fcont[:], m[0:1, 0, 0:1], m[0:1, 1, 0:1], ALU.add)
                    dve.wait_ge(st["dist"], now)
                    nc.vector.tensor_scalar(gap[:], gap[:], 0.0, None, ALU.min).then_inc(st["gap"], 1)
                    dve.wait_ge(st["first_y"], now)
                    nc.vector.scalar_tensor_tensor(fl[:], fy[:], SLOPE, fy[:], ALU.mult, ALU.max).then_inc(st["first_l"], 1)
                    dve.wait_ge(st["first_l"], now)
                    nc.vector.tensor_tensor(fd[:], fl[:], l2[0:1, 0, :], ALU.subtract).then_inc(st["first_d"], 1)
                    if not first:
                        for r in range(REGIONS):
                            add(r, offs[r], past)
                        late_adds(w - 1, (k - 1) % BUFS, slow, past)
                    dve.wait_ge(st["first_d"], now)
                    nc.vector.scalar_tensor_tensor(fdiff[:], fcont[:].to_broadcast([1, H]), -1.0, fd[:], ALU.is_ge, ALU.mult
                                                   ).then_inc(st["fdist"], 1)
                    dve.wait_ge(st["expo"], now)
                    for q in range(4):
                        if q == 1:
                            one_hots(3).then_inc(st["settled"], 1)
                        g4 = slice(4 * q, 4 * q + 4)
                        feats = rows[k][:, g4, 0:D].rearrange("p g (h c) -> p g h c", h=H)
                        nc.vector.tensor_tensor(feats, feats, rows[k][:, g4, D:D + H].unsqueeze(3).to_broadcast([P, 4, H, C]),
                                                ALU.mult).then_inc(st[f"msg{q}"], 1)
                    dve.wait_ge(st["factor"], now)
                    dve.wait_ge(st["settled"], now)
                    num = acc[:, bass.ds(off, D)].rearrange("p (h c) -> p h c", h=H)
                    nc.vector.tensor_tensor(num, num, factor[:].unsqueeze(2).to_broadcast([P, H, C]), ALU.mult)
                    den = acc[:, bass.ds(off + D, H)]
                    nc.vector.tensor_tensor(den, den, factor[:], ALU.mult).then_inc(st["rescaled"], 1)

                nc.vector.memset(inb[:], -BIG)
                for tile in (*passf, *passb):
                    last = nc.vector.memset(tile[:], -BIG)
                last.then_inc(s_start, 1)
                nc.vector.memset(acc[:], 0.0).then_inc(s_clear, 1)
                dve.wait_ge(s_clear, L + 1)
                walk(dve, body)
                *offs, slow = words(dve, 3, (WINDOWS - 1) * WIN, REGIONS + 1)
                for r in range(REGIONS):
                    add(r, offs[r], W0 + WINDOWS)
                late_adds(WINDOWS - 1, (WINDOWS - 1) % BUFS, slow, W0 + WINDOWS, again=False)

    node_phase(None, 0)
    for L in range(3):
        edge_phase(L)
        clear_node_semaphores()
        node_phase(L, L + 1 if L < 2 else None)
    top.close()


def kernel(x, src, dst, L0_gnn_W1, L0_gnn_att_src1, L0_gnn_att_dst1, L0_gnn_b1, L0_gnn_W2, L0_gnn_att_src2,
           L0_gnn_att_dst2, L0_gnn_b2, L1_gnn_W_lin, L1_gnn_b_lin, L1_gnn_W_gat, L1_gnn_attn_l, L1_gnn_attn_r,
           L1_gnn_gat_bias):
    import numpy as np
    import concourse.bacc as bacc
    from concourse.bass_utils import run_bass_kernel_spmd

    def flat_row(a):
        return np.ascontiguousarray(np.asarray(a).reshape(1, -1))

    x = np.asarray(x)
    x_pad = np.zeros((NODES_PAD, D), x.dtype)
    x_pad[:N_NODES] = x
    src, dst = (np.asarray(a) for a in (src, dst))
    src_pad = np.zeros(EDGES_PAD, src.dtype)
    src_pad[:N_EDGES] = src
    dst_pad = np.full(EDGES_PAD + 2, -1, dst.dtype)
    dst_pad[1:-1] = NODES_PAD - 1
    dst_pad[1:N_EDGES + 1] = dst
    edge_tiles = np.concatenate([a.reshape(TILES, P) for a in (src_pad, dst_pad[1:-1], dst_pad[:-2], dst_pad[2:])], axis=1)
    tile_last = np.ascontiguousarray(dst_pad[1:-1].reshape(TILES, P)[:, -1])[None]
    arrays = {
        "x_pad": x_pad, "edge_tiles": edge_tiles, "tile_last": tile_last,
        "w0": np.asarray(L0_gnn_W1), "w1": np.asarray(L0_gnn_W2), "w2": np.asarray(L1_gnn_W_gat),
        "w_lin": np.asarray(L1_gnn_W_lin), "b_lin": flat_row(L1_gnn_b_lin),
        "att0": np.concatenate([flat_row(L0_gnn_att_src1), flat_row(L0_gnn_att_dst1)]),
        "att1": np.concatenate([flat_row(L0_gnn_att_src2), flat_row(L0_gnn_att_dst2)]),
        "att2": np.concatenate([flat_row(L1_gnn_attn_l), flat_row(L1_gnn_attn_r)]),
        "bias0": flat_row(L0_gnn_b1), "bias1": flat_row(L0_gnn_b2), "bias2": flat_row(L1_gnn_gat_bias),
    }
    nc = bacc.Bacc("TRN2", target_bir_lowering=False, num_devices=1)
    t = {n: nc.dram_tensor(f"in_{n}", a.shape, mybir.dt.from_np(a.dtype), kind="ExternalInput").ap()
         for n, a in arrays.items()}
    t["out"] = nc.dram_tensor("result", (N_NODES, D), F32, kind="ExternalOutput").ap()
    build_program(nc, t)
    r = run_bass_kernel_spmd(nc, [{f"in_{n}": a for n, a in arrays.items()}], core_ids=[0])
    return r.results[0]["result"]
```
